# Optimizing a Trainium2 kernel written in Bass

```python
import numpy as np
import jax
import jax.numpy as jnp

def _softmax(x, axis=-1):
    return jax.nn.softmax(x, axis=axis)

def _gelu(x):
    return jax.nn.gelu(x, approximate=True)

def _silu(x):
    return jax.nn.silu(x)

def _sigmoid(x):
    return jax.nn.sigmoid(x)

def _layernorm(x, axis=-1, eps=1e-05):
    m = jnp.mean(x, axis=axis, keepdims=True)
    v = jnp.var(x, axis=axis, keepdims=True)
    return (x - m) / jnp.sqrt(v + eps)

def _scatter_add(tgt, idx, src, axis=0):
    return tgt.at[idx].add(src)

def _segment_sum(src, seg, n):
    return jax.ops.segment_sum(src, seg, n)
kernel_name = 'mk_sandwich_d1_jaxref_r8_84aeef'

def setup_inputs(seed: int=0):
    np.random.seed(seed)
    _w = jnp.asarray

    def _L0_attn_setup():
        import jax, jax.numpy as jnp
        import numpy as np
        N_LAYER, N_HEAD, D_MODEL, D_FF = (6, 16, 128, 512)
        D_HEAD = D_MODEL // N_HEAD
        M_FEAT = 2 * D_MODEL // N_HEAD
        CHUNK = 128
        LN_EPS = 1e-05
        ATT_EPS = 1e-06
        B, S = (4, 256)

        def _layer_norm(x, g, b):
            mu = x.mean(-1, keepdims=True)
            var = ((x - mu) ** 2).mean(-1, keepdims=True)
            return (x - mu) * jax.lax.rsqrt(var + LN_EPS) * g + b

        def _favor_phi(x, omega):
            x = x * D_HEAD ** (-0.25)
            u = jnp.einsum('bhsd,dm->bhsm', x, omega)
            nrm = 0.5 * jnp.sum(x * x, axis=-1, keepdims=True)
            phi = jnp.concatenate([jnp.exp(u - nrm), jnp.exp(-u - nrm)], axis=-1)
            return phi * M_FEAT ** (-0.5)

        def _causal_linear_attention(Qp, Kp, V):
            b, h, s, m = Qp.shape
            d = V.shape[-1]
            c = s // CHUNK
            Qc = Qp.reshape(b, h, c, CHUNK, m)
            Kc = Kp.reshape(b, h, c, CHUNK, m)
            Vc = V.reshape(b, h, c, CHUNK, d)
            kv = jnp.einsum('bhclm,bhcld->bhcmd', Kc, Vc)
            ksum = Kc.sum(axis=3)
            kv_pre = jnp.cumsum(kv, axis=2) - kv
            ks_pre = jnp.cumsum(ksum, axis=2) - ksum
            scores = jnp.einsum('bhcim,bhcjm->bhcij', Qc, Kc)
            mask = jnp.tril(jnp.ones((CHUNK, CHUNK), bool))
            scores = jnp.where(mask, scores, 0.0)
            num = jnp.einsum('bhcij,bhcjd->bhcid', scores, Vc) + jnp.einsum('bhcim,bhcmd->bhcid', Qc, kv_pre)
            den = scores.sum(-1) + jnp.einsum('bhcim,bhcm->bhci', Qc, ks_pre)
            out = num / (den[..., None] + ATT_EPS)
            return out.reshape(b, h, s, d)

        def _forward(x, Wq, bq, Wk, bk, Wv, bv, Wo, bo, omega, g1, be1, W1, bf1, W2, bf2, g2, be2):
            bsz, slen, _ = x.shape
            out = x
            for l in range(N_LAYER):

                def proj(W, bvec):
                    y = jnp.einsum('bsd,de->bse', out, W) + bvec
                    return y.reshape(bsz, slen, N_HEAD, D_HEAD).transpose(0, 2, 1, 3)
                q = proj(Wq[l], bq[l])
                k = proj(Wk[l], bk[l])
                v = proj(Wv[l], bv[l])
                Qp = _favor_phi(q, omega[l])
                Kp = _favor_phi(k, omega[l])
                a = _causal_linear_attention(Qp, Kp, v)
                a = a.transpose(0, 2, 1, 3).reshape(bsz, slen, D_MODEL)
                a = jnp.einsum('bsd,de->bse', a, Wo[l]) + bo[l]
                h1 = _layer_norm(out + a, g1[l], be1[l])
                y = jax.nn.relu(jnp.einsum('bsd,df->bsf', h1, W1[l]) + bf1[l])
                y = jnp.einsum('bsf,fd->bsd', y, W2[l]) + bf2[l]
                out = _layer_norm(h1 + y, g2[l], be2[l])
            return out
        key = jax.random.key(seed)
        ks = jax.random.split(key, 12)
        s = D_MODEL ** (-0.5)
        f32 = jnp.float32
        return {'x': jax.random.normal(ks[0], (B, S, D_MODEL), f32), 'Wq': jax.random.normal(ks[1], (N_LAYER, D_MODEL, D_MODEL), f32) * s, 'bq': jnp.zeros((N_LAYER, D_MODEL), f32), 'Wk': jax.random.normal(ks[2], (N_LAYER, D_MODEL, D_MODEL), f32) * s, 'bk': jnp.zeros((N_LAYER, D_MODEL), f32), 'Wv': jax.random.normal(ks[3], (N_LAYER, D_MODEL, D_MODEL), f32) * s, 'bv': jnp.zeros((N_LAYER, D_MODEL), f32), 'Wo': jax.random.normal(ks[4], (N_LAYER, D_MODEL, D_MODEL), f32) * s, 'bo': jnp.zeros((N_LAYER, D_MODEL), f32), 'omega': jax.random.normal(ks[5], (N_LAYER, D_HEAD, M_FEAT // 2), f32), 'g1': jnp.ones((N_LAYER, D_MODEL), f32), 'be1': jnp.zeros((N_LAYER, D_MODEL), f32), 'W1': jax.random.normal(ks[6], (N_LAYER, D_MODEL, D_FF), f32) * s, 'bf1': jnp.zeros((N_LAYER, D_FF), f32), 'W2': jax.random.normal(ks[7], (N_LAYER, D_FF, D_MODEL), f32) * D_FF ** (-0.5), 'bf2': jnp.zeros((N_LAYER, D_MODEL), f32), 'g2': jnp.ones((N_LAYER, D_MODEL), f32), 'be2': jnp.zeros((N_LAYER, D_MODEL), f32)}
    _L0_attn_in = _L0_attn_setup()

    def _L0_ffn_setup():
        import jax, jax.numpy as jnp
        import numpy as np
        GROUP = 16
        EPS = 1e-05

        def _dequant(q, scale):
            w = q.astype(jnp.float32) / 7.5 - 1.0
            return w * jnp.repeat(scale, GROUP, axis=1)

        def _qlora_linear(x, q, scale, bias, la, lb):
            w = _dequant(q, scale)
            base = jnp.einsum('btd,od->bto', x, w) + bias
            lora = jnp.einsum('btr,or->bto', jnp.einsum('btd,rd->btr', x, la), lb)
            return base + lora

        def _layernorm(x, g, b):
            mu = jnp.mean(x, axis=-1, keepdims=True)
            var = jnp.mean(jnp.square(x - mu), axis=-1, keepdims=True)
            return (x - mu) * jax.lax.rsqrt(var + EPS) * g + b
        key = jax.random.key(seed)
        ks = jax.random.split(key, 6)
        D, R, B, T = (128, 32, 8, 512)
        x = jax.random.normal(ks[0], (B, T, D), dtype=jnp.float32)
        qweights = jax.random.randint(ks[1], (6, D, D), 0, 16, dtype=jnp.int32)
        scales = jax.random.uniform(ks[2], (6, D, D // GROUP), dtype=jnp.float32)
        biases = jax.random.normal(ks[3], (6, D), dtype=jnp.float32) * 0.02
        lora_a = jax.random.normal(ks[4], (6, R, D), dtype=jnp.float32) * 0.02
        lora_b = jax.random.normal(ks[5], (6, D, R), dtype=jnp.float32) * 0.02
        ln_gamma = jnp.ones((3, D), dtype=jnp.float32)
        ln_beta = jnp.zeros((3, D), dtype=jnp.float32)
        return {'x': x, 'qweights': qweights, 'scales': scales, 'biases': biases, 'lora_a': lora_a, 'lora_b': lora_b, 'ln_gamma': ln_gamma, 'ln_beta': ln_beta}
    _L0_ffn_in = _L0_ffn_setup()
    _d = {'L0_attn_x': _L0_attn_in['x'], 'L0_attn_Wq': _L0_attn_in['Wq'], 'L0_attn_bq': _L0_attn_in['bq'], 'L0_attn_Wk': _L0_attn_in['Wk'], 'L0_attn_bk': _L0_attn_in['bk'], 'L0_attn_Wv': _L0_attn_in['Wv'], 'L0_attn_bv': _L0_attn_in['bv'], 'L0_attn_Wo': _L0_attn_in['Wo'], 'L0_attn_bo': _L0_attn_in['bo'], 'L0_attn_omega': _L0_attn_in['omega'], 'L0_attn_g1': _L0_attn_in['g1'], 'L0_attn_be1': _L0_attn_in['be1'], 'L0_attn_W1': _L0_attn_in['W1'], 'L0_attn_bf1': _L0_attn_in['bf1'], 'L0_attn_W2': _L0_attn_in['W2'], 'L0_attn_bf2': _L0_attn_in['bf2'], 'L0_attn_g2': _L0_attn_in['g2'], 'L0_attn_be2': _L0_attn_in['be2'], 'L0_ffn_qweights': _L0_ffn_in['qweights'], 'L0_ffn_scales': _L0_ffn_in['scales'], 'L0_ffn_biases': _L0_ffn_in['biases'], 'L0_ffn_lora_a': _L0_ffn_in['lora_a'], 'L0_ffn_lora_b': _L0_ffn_in['lora_b'], 'L0_ffn_ln_gamma': _L0_ffn_in['ln_gamma'], 'L0_ffn_ln_beta': _L0_ffn_in['ln_beta']}
    _x0 = _d['L0_attn_x']
    _d['L0_attn_x'] = jax.random.normal(jax.random.fold_in(jax.random.key(seed), 1), (4, 1024, 128), dtype=_x0.dtype)
    del _x0
    return _d

def reference(L0_attn_x, L0_attn_Wq, L0_attn_bq, L0_attn_Wk, L0_attn_bk, L0_attn_Wv, L0_attn_bv, L0_attn_Wo, L0_attn_bo, L0_attn_omega, L0_attn_g1, L0_attn_be1, L0_attn_W1, L0_attn_bf1, L0_attn_W2, L0_attn_bf2, L0_attn_g2, L0_attn_be2, L0_ffn_qweights, L0_ffn_scales, L0_ffn_biases, L0_ffn_lora_a, L0_ffn_lora_b, L0_ffn_ln_gamma, L0_ffn_ln_beta):

    def _L0_attn_ref(x, Wq, bq, Wk, bk, Wv, bv, Wo, bo, omega, g1, be1, W1, bf1, W2, bf2, g2, be2):
        import jax, jax.numpy as jnp
        import numpy as np
        N_LAYER, N_HEAD, D_MODEL, D_FF = (6, 16, 128, 512)
        D_HEAD = D_MODEL // N_HEAD
        M_FEAT = 2 * D_MODEL // N_HEAD
        CHUNK = 128
        LN_EPS = 1e-05
        ATT_EPS = 1e-06
        B, S = (4, 256)

        def _layer_norm(x, g, b):
            mu = x.mean(-1, keepdims=True)
            var = ((x - mu) ** 2).mean(-1, keepdims=True)
            return (x - mu) * jax.lax.rsqrt(var + LN_EPS) * g + b

        def _favor_phi(x, omega):
            x = x * D_HEAD ** (-0.25)
            u = jnp.einsum('bhsd,dm->bhsm', x, omega)
            nrm = 0.5 * jnp.sum(x * x, axis=-1, keepdims=True)
            phi = jnp.concatenate([jnp.exp(u - nrm), jnp.exp(-u - nrm)], axis=-1)
            return phi * M_FEAT ** (-0.5)

        def _causal_linear_attention(Qp, Kp, V):
            b, h, s, m = Qp.shape
            d = V.shape[-1]
            c = s // CHUNK
            Qc = Qp.reshape(b, h, c, CHUNK, m)
            Kc = Kp.reshape(b, h, c, CHUNK, m)
            Vc = V.reshape(b, h, c, CHUNK, d)
            kv = jnp.einsum('bhclm,bhcld->bhcmd', Kc, Vc)
            ksum = Kc.sum(axis=3)
            kv_pre = jnp.cumsum(kv, axis=2) - kv
            ks_pre = jnp.cumsum(ksum, axis=2) - ksum
            scores = jnp.einsum('bhcim,bhcjm->bhcij', Qc, Kc)
            mask = jnp.tril(jnp.ones((CHUNK, CHUNK), bool))
            scores = jnp.where(mask, scores, 0.0)
            num = jnp.einsum('bhcij,bhcjd->bhcid', scores, Vc) + jnp.einsum('bhcim,bhcmd->bhcid', Qc, kv_pre)
            den = scores.sum(-1) + jnp.einsum('bhcim,bhcm->bhci', Qc, ks_pre)
            out = num / (den[..., None] + ATT_EPS)
            return out.reshape(b, h, s, d)

        def _forward(x, Wq, bq, Wk, bk, Wv, bv, Wo, bo, omega, g1, be1, W1, bf1, W2, bf2, g2, be2):
            bsz, slen, _ = x.shape
            out = x
            for l in range(N_LAYER):

                def proj(W, bvec):
                    y = jnp.einsum('bsd,de->bse', out, W) + bvec
                    return y.reshape(bsz, slen, N_HEAD, D_HEAD).transpose(0, 2, 1, 3)
                q = proj(Wq[l], bq[l])
                k = proj(Wk[l], bk[l])
                v = proj(Wv[l], bv[l])
                Qp = _favor_phi(q, omega[l])
                Kp = _favor_phi(k, omega[l])
                a = _causal_linear_attention(Qp, Kp, v)
                a = a.transpose(0, 2, 1, 3).reshape(bsz, slen, D_MODEL)
                a = jnp.einsum('bsd,de->bse', a, Wo[l]) + bo[l]
                h1 = _layer_norm(out + a, g1[l], be1[l])
                y = jax.nn.relu(jnp.einsum('bsd,df->bsf', h1, W1[l]) + bf1[l])
                y = jnp.einsum('bsf,fd->bsd', y, W2[l]) + bf2[l]
                out = _layer_norm(h1 + y, g2[l], be2[l])
            return out
        return _forward(x, Wq, bq, Wk, bk, Wv, bv, Wo, bo, omega, g1, be1, W1, bf1, W2, bf2, g2, be2)

    def _L0_ffn_ref(x, qweights, scales, biases, lora_a, lora_b, ln_gamma, ln_beta):
        import jax, jax.numpy as jnp
        import numpy as np
        GROUP = 16
        EPS = 1e-05

        def _dequant(q, scale):
            w = q.astype(jnp.float32) / 7.5 - 1.0
            return w * jnp.repeat(scale, GROUP, axis=1)

        def _qlora_linear(x, q, scale, bias, la, lb):
            w = _dequant(q, scale)
            base = jnp.einsum('btd,od->bto', x, w) + bias
            lora = jnp.einsum('btr,or->bto', jnp.einsum('btd,rd->btr', x, la), lb)
            return base + lora

        def _layernorm(x, g, b):
            mu = jnp.mean(x, axis=-1, keepdims=True)
            var = jnp.mean(jnp.square(x - mu), axis=-1, keepdims=True)
            return (x - mu) * jax.lax.rsqrt(var + EPS) * g + b
        h = x
        for blk in range(3):
            i0, i1 = (2 * blk, 2 * blk + 1)
            y = _qlora_linear(h, qweights[i0], scales[i0], biases[i0], lora_a[i0], lora_b[i0])
            y = _layernorm(y, ln_gamma[blk], ln_beta[blk])
            y = jax.nn.gelu(y, approximate=False)
            y = _qlora_linear(y, qweights[i1], scales[i1], biases[i1], lora_a[i1], lora_b[i1])
            h = y + h
        return h
    x = L0_attn_x
    x = x + _layernorm(_L0_attn_ref(_layernorm(x, axis=-1), L0_attn_Wq, L0_attn_bq, L0_attn_Wk, L0_attn_bk, L0_attn_Wv, L0_attn_bv, L0_attn_Wo, L0_attn_bo, L0_attn_omega, L0_attn_g1, L0_attn_be1, L0_attn_W1, L0_attn_bf1, L0_attn_W2, L0_attn_bf2, L0_attn_g2, L0_attn_be2), axis=-1)
    x = x + _layernorm(_L0_ffn_ref(_layernorm(x, axis=-1), L0_ffn_qweights, L0_ffn_scales, L0_ffn_biases, L0_ffn_lora_a, L0_ffn_lora_b, L0_ffn_ln_gamma, L0_ffn_ln_beta), axis=-1)
    return x

_drawn_inputs = setup_inputs


def setup_inputs(seed=0):
    import zlib

    import numpy as np

    out = dict(_drawn_inputs(seed))
    spreads = {'L0_attn_bq': (0.0, 0.344),
     'L0_attn_bk': (0.0, 0.461),
     'L0_attn_bv': (0.0, 0.1),
     'L0_attn_bo': (0.0, 0.1),
     'L0_attn_g1': (1.0, 0.2),
     'L0_attn_be1': (0.0, 0.1),
     'L0_attn_bf1': (0.0, 0.1),
     'L0_attn_bf2': (0.0, 0.1),
     'L0_attn_g2': (1.0, 0.2),
     'L0_attn_be2': (0.0, 0.1),
     'L0_ffn_ln_gamma': (1.0, 0.2),
     'L0_ffn_ln_beta': (0.0, 0.1)}
    factors = {'L0_ffn_biases': 8.0, 'L0_ffn_lora_a': 8.0, 'L0_ffn_lora_b': 8.0}
    for name, (base, spread) in spreads.items():
        noise = np.random.default_rng([zlib.crc32(name.encode()), seed]).standard_normal(out[name].shape)
        drawn = base * np.exp(spread * noise) if base else spread * noise
        out[name] = jnp.asarray(drawn.astype(out[name].dtype))
    for name, factor in factors.items():
        out[name] = (out[name] * factor).astype(out[name].dtype)
    return out
```

```python
import concourse.bass as bass
from concourse import mybir
from contextlib import ExitStack
import numpy as np

F32 = mybir.dt.float32
I32 = mybir.dt.int32
ACT = mybir.ActivationFunctionType
ALU = mybir.AluOpType

LAYERS, HEADS, D, FF, DH, M2 = 6, 16, 128, 512, 8, 8
SEQ, NBLK, CH = 4, 8, 128
TOK = SEQ * CH
TASKS = LAYERS * NBLK
HT_ = HEADS // 2
SLOT = 16
FT = FF // 128
QBLK = 3
LN_EPS = 1e-5
DEN_EPS = 16 * 1e-6
S_X = float(DH) ** -0.25
DEN = 8

RA = 3 * 128 + 2
RC = FF + FT

STEPS = [("T0", 5, "C"), ("T1", 6, "C"), ("QP", 7, "A"), ("KP", 5, "A"), ("AT", 6, "C"), ("LQ0", 7, "A"),
         ("LQ1", 5, "A"), ("WO", 6, "C"), ("LK0", 7, "A"), ("LK1", 5, "A"), ("XD", 6, "D"), ("VP", 7, "A"),
         ("HT", 5, "C"), ("W1_0", 6, "C"), ("W1_1", 7, "C"), ("W1_2", 5, "C"), ("W1_3", 6, "C"),
         ("W2", 6, "C"), ("KT0", 7, "A"), ("KT1", 5, "A")]
LAG = {"A": 1, "B": 0, "C": -1, "D": -2}
FIRST, LAST = -1, TASKS + 1
LOOP0, LOOPS = 3, (TASKS - 3 - 3) // 2
BANK = {s: b for s, b, _ in STEPS}


class It:

    def __init__(self, base, k=None):
        self.base, self.k = base, k

    def val(self, rate, off):
        v = rate * self.base + off
        return v if self.k is None else self.k * (2 * rate) + v

    def active(self, stage):
        return 0 <= self.base + LAG[stage] < TASKS

    def par(self, stage):
        return (self.base + LAG[stage]) % 2

    def layer(self, stage):
        b = self.val(1, LAG[stage])
        return b // NBLK

    def blk(self, stage):
        b = self.val(1, LAG[stage])
        return b % NBLK

    def prev(self):
        return It(self.base - 1, self.k)


def fills(step, it):
    bank, n = BANK[step], 0
    for s, b, stage in STEPS:
        if b != bank:
            continue
        upto = it.base if [x[0] for x in STEPS].index(s) <= [x[0] for x in STEPS].index(step) else it.base - 1
        n += max(0, min(upto + LAG[stage], TASKS - 1) + 1)
    if it.k is None:
        return n
    assert it.base >= 2
    return it.k * (2 * sum(b == bank for _, b, _ in STEPS)) + n


def wait(eng, sem, value):
    if isinstance(value, int) and value <= 0:
        return
    eng.wait_ge(sem, value)


def wait_apart(eng, sem, value, scratch):
    wait(eng, sem, value)
    eng.memset(scratch, 0.0)


def sandwich(nc, x, Wq, bq, Wk, bk, Wv, bv, Wo, bo, omega, g1, be1, W1, bf1, W2, bf2, g2, be2,
             qw, qscale, qbias, lora_a, lora_b, ln_g, ln_b, out):
    ctx = ExitStack()

    def sb(name, shape, dt=F32):
        return ctx.enter_context(nc.sbuf_tensor(name, shape, dt))

    def sem(name):
        return ctx.enter_context(nc.semaphore(name))

    with ctx:
        XT = sb("x_feat", [128, NBLK, TOK])
        XK = sb("x_tok", [128, NBLK, SEQ, D])
        WA = sb("w_rec_a", [128, LAYERS, RA])
        WC = sb("w_rec_c", [128, LAYERS, RC])
        WV = sb("w_v", [128, LAYERS, D])
        WO = sb("w_o", [128, LAYERS, D])
        WD = sb("w_2", [128, LAYERS, FT, D])
        BV = sb("bv_rows", [128, LAYERS, D])
        BO = sb("bo_rows", [128, LAYERS + 1, D])
        G1 = sb("g1_rows", [128, LAYERS, D])
        BE1 = sb("be1_rows", [128, LAYERS, D])
        BF2 = sb("bf2_rows", [128, LAYERS, D])
        G2 = sb("g2_rows", [128, LAYERS, D])
        BE2 = sb("be2_rows", [128, LAYERS, D])
        WE = sb("w_eff", [128, 2 * QBLK, D])
        QB = sb("q_bias_rows", [128, 2 * QBLK, D])
        QG = sb("q_gamma_beta", [128, 2, QBLK])
        IDN = sb("identity", [128, 128])
        TRI = sb("causal", [128, 128])
        BDM = sb("head_blocks", [128, 128])
        HM8 = sb("head_of_row", [128, HT_])
        PARM = sb("head_parity", [128, 2])
        KEEP = sb("keep_state", [128, TASKS + 1])
        NHALF = sb("minus_half", [128, 32])
        CA = sb("cur_a", [128, RA])
        CC = sb("cur_c", [128, RC])
        XS = sb("x_feat_cur", [128, TOK])
        PQ = sb("phi_q", [128, 2, 2, TOK])
        PK = sb("phi_k", [128, 2, TOK])
        KP = sb("phi_k_by_parity", [128, 2, 2, 2, TOK])
        KTK = sb("phi_k_tok", [128, SEQ, 2, 128])
        VP = sb("v_padded", [128, 2, SEQ, HEADS, 32])
        SM = sb("scores_masked", [128, 2, 4, 4, CH])
        SF = sb("state_full", [128, SEQ, 2, 128])
        SK = sb("state_masked", [128, SEQ, 2, 128])
        MK = sb("keep_blocks", [128, 128])
        OS = sb("attn_num_den", [128, SEQ, 2, CH])
        DN = sb("den", [128, 2, 32])
        AK = sb("attn_tok", [128, SEQ, D])
        AF = sb("attn_feat", [128, TOK])
        R = sb("ln_in", [128, SEQ, D])
        N = sb("ln_out", [128, SEQ, D])
        ST = sb("ln_stats", [128, SEQ, 6])
        MV = sb("ln_mean_var", [128, SEQ, 2])
        VE = sb("ln_var_eps", [128, SEQ])
        RS = sb("ln_rstd", [128, SEQ])
        H1 = sb("h1_tok", [128, SEQ, D])
        H1B = sb("h1_bias_tok", [128, SEQ, D])
        HF = sb("h1_feat", [128, TOK])
        Y = sb("ff_feat", [128, FT, TOK])
        QS = Y
        X2 = sb("x_tok_cur", [128, SEQ, D])
        CARRY = sb("wait_carrier", [128, 2])
        MVA = sb("ln_mean_var_all", [128, NBLK, SEQ, 2])
        VEA = sb("ln_var_eps_all", [128, NBLK * SEQ])
        RSA = sb("ln_rstd_all", [128, NBLK * SEQ])
        P = ctx.enter_context(nc.psum_tensor("banks", [128, 8, 512], F32))

        def rows(table, l):
            return table[:, l, :].unsqueeze(1).to_broadcast([128, SEQ, D])

        x_dram = [x[s].rearrange("(p i) f -> i p f", i=CH) for s in range(SEQ)]
        out_dram = [out[s].rearrange("(p i) f -> i p f", i=CH) for s in range(SEQ)]

        x_in = sem("x_in"); w_in = sem("w_in"); q_in = sem("q_in"); om_in = sem("om_in")
        consts = sem("consts"); cst_step = sem("cst_step")
        pre_stats = sem("pre_stats"); pre_aggr = sem("pre_aggr"); pre_mv = sem("pre_mv"); pre_var = sem("pre_var"); pre_rstd = sem("pre_rstd")
        pre_norm = sem("pre_norm"); pre_t = sem("pre_t"); pre_xt = sem("pre_xt"); pre_xk = sem("pre_xk")
        om_step = sem("om_step"); dq_step = sem("dq_step"); lb_t = sem("lb_t"); lb_sb = sem("lb_sb")
        we_ps = sem("we_ps"); we_sb = sem("we_sb"); bias_done = sem("bias_done")

        OMR = Y[0:64, 0, 0:LAYERS * M2].rearrange("p (l m) -> p l m", l=LAYERS)
        QI = SM[:, 0, 0:2].rearrange("p a b c -> p (a b c)")[:, 0:2 * QBLK * D] \
            .rearrange("p (w d) -> p w d", w=2 * QBLK).bitcast(I32)
        QW = SM[:, 0, 2:4].rearrange("p a b c -> p (a b c)")[:, 0:2 * QBLK * D] \
            .rearrange("p (w d) -> p w d", w=2 * QBLK)
        QSC = Y[:, 1, 0:48].rearrange("p (w g) -> p w g", w=6)
        LA = SM[0:32, 1, 0:2].rearrange("p a b c -> p (a b c)")[:, 0:768].rearrange("p (w d) -> p w d", w=6)
        LB = Y[:, 2, 0:192].rearrange("p (w r) -> p w r", w=6)
        LBT = SM[0:32, 1, 2:4].rearrange("p a b c -> p (a b c)")[:, 0:768].rearrange("p (w d) -> p w d", w=6)

        with nc.Block() as block:
            @block.sync
            def _(sp):
                for s in (0, 1):
                    sp.dma_start(XK[:, :, s, :], x_dram[s]).then_inc(x_in, 16)
                sp.dma_start(WA[:, :, 0:128], Wq.rearrange("l d e -> d l e")).then_inc(w_in, 16)
                sp.dma_start(WA[:, :, 128:256], Wk.rearrange("l d e -> d l e")).then_inc(w_in, 16)
                sp.dma_start(WV[:, :, :], Wv.rearrange("l d e -> d l e")).then_inc(w_in, 16)
                sp.dma_start(WO[:, :, :], Wo.rearrange("l d e -> d l e")).then_inc(w_in, 16)
                sp.dma_start(WC[:, :, 0:FF], W1.rearrange("l d f -> d l f")).then_inc(w_in, 16)
                for t in range(FT):
                    sp.dma_start(WD[:, :, t, :], W2[:, 128 * t:128 * t + 128, :].rearrange("l f d -> f l d")) \
                        .then_inc(w_in, 16)
                sp.dma_start(QI, qw.rearrange("w o d -> o w d")).then_inc(q_in, 16)
                sp.dma_start(QSC, qscale.rearrange("w o g -> o w g")).then_inc(q_in, 16)
                sp.dma_start(LA, lora_a.rearrange("w r d -> r w d")).then_inc(q_in, 16)
                sp.dma_start(LB, lora_b.rearrange("w o r -> o w r")).then_inc(q_in, 16)
                sp.wait_ge(w_in, 16 * 25)
                sp.wait_ge(q_in, 64)

            @block.scalar
            def _(act):
                for s in (2, 3):
                    act.dma_start(XK[:, :, s, :], x_dram[s]).then_inc(x_in, 16)
                for h in range(HT_):
                    act.dma_start(OMR[8 * h:8 * h + 8], omega.rearrange("l d m -> d l m")).then_inc(om_in, 16)
                for table, src in ((BV, bv), (BO, bo), (G1, g1), (BE1, be1), (BF2, bf2), (G2, g2), (BE2, be2)):
                    act.dma_start(table[:, 0:LAYERS, :], src.partition_broadcast(128)).then_inc(w_in, 16)
                act.dma_start(QB[:, :, :], qbias.partition_broadcast(128)).then_inc(w_in, 16)
                with nc.allow_non_contiguous_dma(reason="small tables by feature"):
                    act.dma_start(WA[:, :, 384], bq.rearrange("l e -> e l")).then_inc(w_in, 16)
                    act.dma_start(WA[:, :, 385], bk.rearrange("l e -> e l")).then_inc(w_in, 16)
                    for t in range(FT):
                        act.dma_start(WC[:, :, FF + t], bf1[:, 128 * t:128 * t + 128].rearrange("l f -> f l")) \
                            .then_inc(w_in, 16)
                    act.dma_start(QG[:, 0, :], ln_g.rearrange("l f -> f l")).then_inc(w_in, 16)
                    act.dma_start(QG[:, 1, :], ln_b.rearrange("l f -> f l")).then_inc(w_in, 16)
                with act.Fori(0, NBLK) as p:
                    act.wait_ge(pre_t, p + 1)
                    nc.scalar.activation(XT[:, p, :], P[:, 0, :], ACT.Copy).then_inc(pre_xt, 1)
                for w in range(2 * QBLK):
                    act.wait_ge(lb_t, w + 1)
                    nc.scalar.activation(LBT[:, w, :], P[0:32, 1, 0:128], ACT.Copy).then_inc(lb_sb, 1)
                for w in range(2 * QBLK):
                    act.wait_ge(we_ps, w + 1)
                    nc.scalar.activation(WE[:, w, :], P[:, 2, 0:128], ACT.Copy).then_inc(we_sb, 1)

            @block.gpsimd
            def _(pool):
                def select(t, op, pattern, base, mult, fill, n):
                    pool.wait_ge(cst_step, n)
                    pool.affine_select(out=t, in_=t, compare_op=op, fill=fill, base=base, pattern=pattern,
                                       channel_multiplier=mult).then_inc(cst_step, 1)

                pool.memset(IDN[:, :], 0.0).then_inc(cst_step, 1)
                pool.memset(TRI[:, :], 1.0).then_inc(cst_step, 1)
                pool.memset(BDM[:, :], 1.0).then_inc(cst_step, 1)
                pool.memset(HM8[:, :], 1.0).then_inc(cst_step, 1)
                pool.memset(PARM[:, :], 0.0).then_inc(cst_step, 1)
                pool.memset(KEEP[:, :], 1.0).then_inc(cst_step, 1)
                select(IDN[:, :], ALU.not_equal, [[-1, 128]], 0, 1, 1.0, 6)
                select(TRI[:, :], ALU.is_ge, [[1, 128]], 0, -1, 0.0, 7)
                bdm = BDM[:, :].rearrange("p (h c) -> p h c", h=HT_)
                select(bdm, ALU.is_ge, [[-SLOT, HT_], [0, SLOT]], 0, 1, 0.0, 8)
                select(bdm, ALU.is_ge, [[SLOT, HT_], [0, SLOT]], SLOT - 1, -1, 0.0, 9)
                for half in range(2):
                    hm = HM8[64 * half:64 * half + 64, :]
                    select(hm, ALU.is_ge, [[-DH, HT_]], 0, 1, 0.0, 10 + 2 * half)
                    select(hm, ALU.is_ge, [[DH, HT_]], DH - 1, -1, 0.0, 11 + 2 * half)
                pool.wait_ge(cst_step, 14)
                for par in range(2):
                    for g in range(4):
                        h = 2 * g + par
                        pool.tensor_tensor(PARM[:, par:par + 1], PARM[:, par:par + 1],
                                           BDM[:, SLOT * h:SLOT * h + 1], ALU.add).then_inc(cst_step, 1)
                        pool.wait_ge(cst_step, 15 + 4 * par + g)
                pool.memset(KEEP[:, 0:TASKS + 1:NBLK], 0.0).then_inc(consts, 1)
                pool.memset(NHALF[:, :], -0.5).then_inc(consts, 1)
                pool.memset(BO[:, LAYERS, :], 0.0).then_inc(consts, 1)
                pool.memset(VP[:, :, :, :, :], 0.0).then_inc(cst_step, 1)
                pool.memset(SK[:, :, :, :], 0.0).then_inc(cst_step, 1)
                pool.memset(SF[:, :, :, :], 0.0).then_inc(cst_step, 1)
                pool.wait_ge(cst_step, 25)
                for buf in range(2):
                    for s in range(SEQ):
                        for par in range(2):
                            ones = VP[:, buf, s, par::2, SLOT * par + DEN]
                            pool.memset(ones, 1.0).then_inc(cst_step, 1)
                pool.wait_ge(consts, 3)
                pool.wait_ge(pre_var, 1)
                pool.tensor_tensor(RSA[:, :], VEA[:, :], NHALF[:, :], ALU.pow).then_inc(pre_rstd, 1)
                pool.wait_ge(w_in, 16 * 25)
                with pool.Fori(0, NBLK) as p:
                    pool.wait_ge(pre_norm, p + 1)
                    pool.tensor_tensor(XK[:, p], X2[:, :, :], rows(BO, 0), ALU.add).then_inc(pre_xk, 1)

            @block.vector
            def _(dve):
                dve.wait_ge(x_in, 64)
                with dve.Fori(0, NBLK) as p:
                    for s in range(SEQ):
                        nc.vector.bn_stats(ST[:, s, :], XK[:, p, s, :]).then_inc(pre_stats, 1)
                    wait_apart(dve, pre_stats, p * SEQ + SEQ, CARRY[:, 0:1])
                    for s in range(SEQ):
                        nc.vector.bn_aggr(MV[:, s, :], ST[:, s, :]).then_inc(pre_aggr, 1)
                    dve.wait_ge(pre_aggr, p * SEQ + SEQ)
                    nc.vector.tensor_copy(MVA[:, p], MV[:, :, :]).then_inc(pre_mv, 1)
                dve.wait_ge(pre_mv, NBLK)
                nc.vector.tensor_scalar(VEA[:, :], MVA[:, :, :, 1].rearrange("p a b -> p (a b)"), LN_EPS, None,
                                        ALU.add).then_inc(pre_var, 1)
                dve.wait_ge(pre_rstd, 1)

                def norm_block(p):
                    wait(dve, pre_t, p)
                    wait(dve, pre_xk, p)
                    for s in range(SEQ):
                        ins = nc.vector.tensor_scalar(X2[:, s, :], XK[:, p, s, :], MVA[:, p, s, 0:1],
                                                      RSA[:, bass.ds(p * SEQ + s, 1)], ALU.subtract, ALU.mult)
                    ins.then_inc(pre_norm, 1)

                norm_block(0)
                with dve.Fori(1, NBLK) as p:
                    norm_block(p)
                dve.wait_ge(om_in, 16 * HT_)
                dve.wait_ge(cst_step, 14)
                for l in range(LAYERS):
                    om = WA[:, l, 256:384].rearrange("p (h g m) -> p h g m", h=HT_, g=2)
                    nc.vector.tensor_tensor(om[0:64, :, 0, :], OMR[:, l, :].unsqueeze(1).to_broadcast([64, HT_, M2]),
                                            HM8[0:64, :].unsqueeze(2).to_broadcast([64, HT_, M2]),
                                            ALU.mult).then_inc(om_step, 1)
                dve.wait_ge(om_step, LAYERS)
                for l in range(LAYERS):
                    om = WA[:, l, 256:384].rearrange("p (h g m) -> p h g m", h=HT_, g=2)
                    nc.vector.tensor_scalar(om[0:64, :, 1, :], om[0:64, :, 0, :], -1.0, None, ALU.mult)
                    nc.vector.tensor_scalar(WA[64:128, l, 256:384].rearrange("p (h c) -> p h c", h=HT_),
                                            HM8[64:128, :].unsqueeze(2).to_broadcast([64, HT_, 2 * M2]),
                                            -0.5, None, ALU.mult)
                dve.wait_ge(w_in, 16 * 25)
                nc.vector.tensor_scalar(WA[:, :, 384:386], WA[:, :, 384:386], S_X, None, ALU.mult) \
                    .then_inc(bias_done, 1)
                dve.wait_ge(q_in, 64)
                nc.vector.tensor_scalar(QW, QI, 1.0 / 7.5, -1.0, ALU.mult, ALU.add).then_inc(dq_step, 1)
                dve.wait_ge(dq_step, 1)
                for w in range(2 * QBLK):
                    v = QW[:, w, :].rearrange("p (g c) -> p g c", c=16)
                    nc.vector.tensor_tensor(v, v, QSC[:, w, :].unsqueeze(2).to_broadcast([128, 8, 16]), ALU.mult) \
                        .then_inc(dq_step, 1)

            @block.tensor
            def _(pe):
                pe.wait_ge(cst_step, 7)

                def transpose_block(p):
                    wait(pe, pre_norm, p + 1)
                    wait(pe, pre_xt, p)
                    for s in range(SEQ):
                        ins = nc.tensor.transpose(P[:, 0, CH * s:CH * s + CH], X2[:, s, :], IDN[:, :])
                    ins.then_inc(pre_t, 1)

                transpose_block(0)
                with pe.Fori(1, NBLK) as p:
                    transpose_block(p)
                pe.wait_ge(q_in, 64)
                for w in range(2 * QBLK):
                    wait(pe, lb_sb, w)
                    nc.tensor.transpose(P[0:32, 1, 0:128], LB[:, w, :], IDN[:, :]).then_inc(lb_t, 1)
                for w in range(2 * QBLK):
                    pe.wait_ge(dq_step, w + 2)
                    pe.wait_ge(lb_sb, 2 * QBLK)
                    wait(pe, we_sb, w)
                    nc.tensor.matmul(P[:, 2, 0:128], QW[:, w, :], IDN[:, :], start=True, stop=False)
                    nc.tensor.matmul(P[:, 2, 0:128], LA[:, w, :], LBT[:, w, :], start=False, stop=True) \
                        .then_inc(we_ps, 1)

        filled = {b: sem(f"bank{b}_filled") for b in (5, 6, 7)}
        drained = {b: sem(f"bank{b}_drained") for b in (5, 6, 7)}
        scores_full = sem("scores_full")
        scores_masked = sem("scores_masked")
        av_done = sem("av_done")
        o_copied = sem("o_copied")
        state_full = sem("state_full")
        state_added = sem("state_added")
        state_ready = sem("state_ready")
        keep_ready = sem("keep_ready")
        kp_ready = sem("kp_ready")
        xs_ready = sem("xs_ready")
        wa_ready = sem("wa_ready")
        wc_ready = sem("wc_ready")
        den_step = sem("den_step")
        ln_in = sem("ln_in_ready")
        ln_stats = sem("ln_stats_ready")
        ln_mv = sem("ln_mean_var_ready")
        ln_var = sem("ln_var_eps_ready")
        ln_rstd = sem("ln_rstd_ready")
        ln_norm = sem("ln_norm_ready")
        ln_gain = sem("ln_gain_ready")
        ln_out = sem("ln_out_ready")
        h1b_ready = sem("h1b_ready")
        xk_ready = sem("xk_ready")

        def full(eng, step, it):
            wait(eng, filled[BANK[step]], fills(step, it))

        def emptied(eng, step, it):
            wait(eng, drained[BANK[step]], fills(step, it))

        def claim(eng, step, it):
            n = fills(step, it)
            wait(eng, drained[BANK[step]], n - 1 if isinstance(n, int) else n + -1)

        def pipeline(eng, body):
            for m in range(FIRST, LOOP0):
                body(It(m))
            with eng.Fori(0, LOOPS) as k:
                for par in range(2):
                    body(It(LOOP0 + par, k))
            for m in range(LOOP0 + 2 * LOOPS, LAST + 1):
                body(It(m))

        def v_dense(par, s, t):
            return VP[:, par, s, HT_ * t:HT_ * t + HT_, :].rearrange("p (a b) (q c) -> p a (b q) c", b=2, c=SLOT)[:, :, 0::3, :]

        def bank4(s):
            return P[:, 4, 256 * (s % 2):256 * (s % 2) + 256].rearrange("p (t i) -> p t i", t=2)

        with nc.Block() as block:
            @block.tensor
            def _(pe):
                def fill(step, it, ins):
                    ins.then_inc(filled[BANK[step]], 1)

                def scores(it, s):
                    par = it.par("B")
                    if s == 0:
                        emptied(pe, "LQ1", it.prev())
                        wait(pe, kp_ready, it.val(4, 4))
                    for sub in range(4):
                        for g in range(4):
                            if sub == 0:
                                wait(pe, scores_masked, it.val(16, 4 * (s - 1) + g + 1))
                            rg = slice(32 * g, 32 * g + 32)
                            ins = nc.tensor.matmul(P[:, g, CH * sub:CH * sub + CH],
                                                   KP[rg, par, sub // 2, sub % 2, CH * s:CH * s + CH],
                                                   PQ[rg, par, sub // 2, CH * s:CH * s + CH],
                                                   start=True, stop=True, skip_group_check=True)
                    ins.then_inc(scores_full, 1)

                def attend(it, s):
                    par = it.par("B")
                    o = bank4(s)
                    if s == 0:
                        emptied(pe, "VP", it.prev())
                        wait(pe, state_ready, it.val(2, 0))
                        wait(pe, state_added, it.val(2, 0))
                    if s == 2:
                        wait(pe, state_added, it.val(2, 1))
                    for t in range(2):
                        nc.tensor.matmul(o[:, t, :], SK[:, s, t, :], PQ[:, par, t, CH * s:CH * s + CH],
                                         start=(t == 0), stop=False, skip_group_check=True)
                    wait(pe, scores_masked, it.val(16, 4 * s + 4))
                    for sub in range(4):
                        for g in range(4):
                            t, h = sub // 2, 8 * (sub // 2) + 2 * g + sub % 2
                            ins = nc.tensor.matmul(o[32 * g:32 * g + 32, t, :], VP[:, par, s, h, :],
                                                   SM[:, s % 2, g, sub, :], start=False, stop=(sub % 2 == 1),
                                                   skip_group_check=True)
                    ins.then_inc(av_done, 1)

                def state(it, j):
                    par = it.par("B")
                    if j == 0:
                        emptied(pe, "KT1", it.prev())
                    wait(pe, o_copied, it.val(2, 1 + j))
                    for s in (2 * j, 2 * j + 1):
                        for t in range(2):
                            ins = nc.tensor.matmul(bank4(s)[:, t, :], KTK[:, s, t, :], v_dense(par, s, t),
                                                   start=True, stop=True, skip_group_check=True)
                    ins.then_inc(state_full, 1)

                def project(it, step, col):
                    claim(pe, step, it)
                    if step == "QP":
                        wait(pe, wa_ready, it.val(1, 2))
                        emptied(pe, "XD", it.prev())
                    fill(step, it, nc.tensor.matmul(P[:, BANK[step], :], CA[:, col:col + 128],
                                                    XT[:, it.blk("A"), :], start=True, stop=True))

                def logits(it, step, n):
                    claim(pe, step, it)
                    emptied(pe, "QP" if n < 2 else "KP", it)
                    fill(step, it, nc.tensor.matmul(P[:, BANK[step], :], CA[:, 256:384], QS[:, n, :],
                                                    start=True, stop=True))

                def transposes(it, step, srcs):
                    claim(pe, step, it)
                    for n, src in enumerate(srcs):
                        ins = nc.tensor.transpose(P[:, BANK[step], CH * n:CH * n + CH], src, IDN[:, :])
                    fill(step, it, ins)

                def body(it):
                    A, B, C, Dd = (it.active(x) for x in "ABCD")
                    if B:
                        scores(it, 0)
                    if C:
                        for j in range(2):
                            wait(pe, o_copied, it.val(2, j - 1))
                            transposes(it, f"T{j}", [OS[:, s, t, :] for s in (2 * j, 2 * j + 1) for t in range(2)])
                    if A:
                        project(it, "QP", 0)
                        project(it, "KP", 128)
                    if B:
                        scores(it, 1)
                    if C:
                        emptied(pe, "T0", it)
                        emptied(pe, "T1", it)
                        transposes(it, "AT", [AK[:, s, :] for s in range(SEQ)])
                    if B:
                        attend(it, 0)
                    if A:
                        logits(it, "LQ0", 0)
                        logits(it, "LQ1", 1)
                    if C:
                        claim(pe, "WO", it)
                        emptied(pe, "AT", it)
                        for s in range(SEQ):
                            ins = nc.tensor.matmul(P[:, BANK["WO"], CH * s:CH * s + CH], AF[:, CH * s:CH * s + CH],
                                                   WO[:, it.layer("C"), :], start=True, stop=True)
                        fill("WO", it, ins)
                    if A:
                        logits(it, "LK0", 2)
                        logits(it, "LK1", 3)
                    if B:
                        scores(it, 2)
                        attend(it, 1)
                    if Dd:
                        wait(pe, ln_out, it.val(2, -2))
                        transposes(it, "XD", [X2[:, s, :] for s in range(SEQ)])
                    if A:
                        claim(pe, "VP", it)
                        wait(pe, xs_ready, it.val(1, 2))
                        for s in range(SEQ):
                            ins = nc.tensor.matmul(P[:, BANK["VP"], CH * s:CH * s + CH], XS[:, CH * s:CH * s + CH],
                                                   WV[:, it.layer("A"), :], start=True, stop=True)
                        fill("VP", it, ins)
                    if B:
                        state(it, 0)
                    if C:
                        wait(pe, ln_out, it.val(2, -1))
                        transposes(it, "HT", [H1[:, s, :] for s in range(SEQ)])
                    if B:
                        scores(it, 3)
                        attend(it, 2)
                    if C:
                        wait(pe, wc_ready, it.val(1, 0))
                        emptied(pe, "HT", it)
                        for f in range(FT):
                            step = f"W1_{f}"
                            claim(pe, step, it)
                            fill(step, it, nc.tensor.matmul(P[:, BANK[step], :], CC[:, 128 * f:128 * f + 128],
                                                            HF[:, :], start=True, stop=True))
                    if B:
                        attend(it, 3)
                    if C:
                        claim(pe, "W2", it)
                        for s in range(SEQ):
                            for f in range(FT):
                                ins = nc.tensor.matmul(P[:, BANK["W2"], CH * s:CH * s + CH],
                                                       Y[:, f, CH * s:CH * s + CH], WD[:, it.layer("C"), f, :],
                                                       start=(f == 0), stop=(f == FT - 1))
                        fill("W2", it, ins)
                    if B:
                        state(it, 1)
                    if A:
                        emptied(pe, "LK0", it)
                        emptied(pe, "LK1", it)
                        for j in range(2):
                            transposes(it, f"KT{j}", [PK[:, t, CH * s:CH * s + CH]
                                                      for s in (2 * j, 2 * j + 1) for t in range(2)])

                pipeline(pe, body)

            @block.scalar
            def _(act):
                def copy_out(it, step, dst, func=ACT.Copy, **kw):
                    full(act, step, it)
                    nc.scalar.activation(dst, P[:, BANK[step], :], func, **kw).then_inc(drained[BANK[step]], 1)

                def lines_squares(it, step, n):
                    full(act, step, it)
                    src, col = P[:, BANK[step], :], 384 + n
                    for half in range(2):
                        hr = slice(64 * half, 64 * half + 64)
                        nc.scalar.activation(QS[0:64, 2 * n + half, :], src[hr, :], ACT.Identity,
                                             bias=CA[hr, col:col + 1], scale=S_X)
                        ins = nc.scalar.activation(QS[64:128, 2 * n + half, :], src[hr, :], ACT.Square,
                                                   bias=CA[hr, col:col + 1], scale=S_X)
                    ins.then_inc(drained[BANK[step]], 1)

                def attn_copy(it, j):
                    wait(act, av_done, it.val(4, 2 * j + 2))
                    nc.scalar.activation(OS[:, 2 * j:2 * j + 2].rearrange("p a b c -> p (a b c)"), P[:, 4, :],
                                         ACT.Copy).then_inc(o_copied, 1)

                def body(it):
                    A, B, C, Dd = (it.active(x) for x in "ABCD")
                    if A:
                        lines_squares(it, "QP", 0)
                        lines_squares(it, "KP", 1)
                    if C:
                        copy_out(it, "AT", AF[:, :])
                    if A:
                        copy_out(it, "LQ0", PQ[:, it.par("A"), 0, :], ACT.Exp)
                        copy_out(it, "LQ1", PQ[:, it.par("A"), 1, :], ACT.Exp)
                        wait(act, kp_ready, it.val(4, 4))
                        copy_out(it, "LK0", PK[:, 0, :], ACT.Exp)
                        copy_out(it, "LK1", PK[:, 1, :], ACT.Exp)
                        if it.base + 2 < TASKS:
                            emptied(act, "KP", it)
                            nc.scalar.activation(CA[:, :], WA[:, it.val(1, 2) // NBLK, :], ACT.Copy) \
                                .then_inc(wa_ready, 1)
                    if B:
                        attn_copy(it, 0)
                    if Dd:
                        copy_out(it, "XD", XT[:, it.blk("D"), :])
                    if C:
                        copy_out(it, "HT", HF[:, :])
                        for f in range(FT):
                            copy_out(it, f"W1_{f}", Y[:, f, :], ACT.Relu, bias=CC[:, FF + f:FF + f + 1])
                    if B:
                        emptied(act, "W1_2", it)
                        emptied(act, "W1_3", it)
                        nc.scalar.activation(CC[:, :], WC[:, it.val(1, 0) // NBLK, :], ACT.Copy).then_inc(wc_ready, 1)
                        attn_copy(it, 1)
                    if A:
                        for j in range(2):
                            copy_out(it, f"KT{j}", KTK[:, 2 * j:2 * j + 2].rearrange("p a b c -> p (a b c)"))

                nc.scalar.activation(CA[:, :], WA[:, 0, :], ACT.Copy).then_inc(wa_ready, 1)
                pipeline(act, body)

            @block.vector
            def _(dve):
                def mask(it, s):
                    wait(dve, scores_full, it.val(4, s + 1))
                    wait(dve, av_done, it.val(4, s - 1))
                    for g in range(4):
                        nc.vector.tensor_tensor(SM[:, s % 2, g, :, :], P[:, g, :].rearrange("p (a i) -> p a i", a=4),
                                                TRI[:, :].unsqueeze(1).to_broadcast([128, 4, 128]),
                                                ALU.mult).then_inc(scores_masked, 1)

                def divide(it, j):
                    full(dve, f"T{j}", it)
                    t = P[:, BANK[f"T{j}"], :].rearrange("p (h c) -> p h c", c=SLOT)
                    nc.vector.tensor_scalar(DN[:, 0, :], t[:, :, DEN], DEN_EPS, None, ALU.add).then_inc(den_step, 1)
                    wait(dve, den_step, it.val(4, 2 * j - 3))
                    nc.vector.reciprocal(DN[:, 1, :], DN[:, 0, :]).then_inc(den_step, 1)
                    wait(dve, den_step, it.val(4, 2 * j - 2))
                    nc.vector.tensor_tensor(AK[:, 2 * j:2 * j + 2, :].rearrange("p s (h d) -> p (s h) d", d=DH),
                                            t[:, :, 0:DH], DN[:, 1, :].unsqueeze(2).to_broadcast([128, 32, DH]),
                                            ALU.mult).then_inc(drained[BANK[f"T{j}"]], 1)

                def statistics(it, n):
                    for s in range(SEQ):
                        nc.vector.bn_stats(ST[:, s, :], R[:, s, :]).then_inc(ln_stats, 1)
                    wait_apart(dve, ln_stats, it.val(8, 4 * n - 8), CARRY[:, 0:1])
                    for s in range(SEQ):
                        nc.vector.bn_aggr(MV[:, s, :], ST[:, s, :]).then_inc(ln_mv, 1)
                    wait(dve, ln_mv, it.val(8, 4 * n - 8))
                    nc.vector.tensor_scalar(VE[:, :], MV[:, :, 1], LN_EPS, None, ALU.add).then_inc(ln_var, 1)

                def normalise(it, n):
                    wait(dve, ln_rstd, it.val(2, n - 2))
                    wait(dve, ln_out, it.val(2, n - 3))
                    for s in range(SEQ):
                        ins = nc.vector.tensor_scalar(N[:, s, :], R[:, s, :], MV[:, s, 0:1], RS[:, s:s + 1],
                                                      ALU.subtract, ALU.mult)
                    ins.then_inc(ln_norm, 1)

                def add_state(it, j):
                    wait(dve, state_full, it.val(2, 1 + j))
                    wait(dve, state_ready, it.val(2, j - 1))
                    m = it.val(1, 0)
                    sf = SF[:, 2 * j:2 * j + 2].rearrange("p a b c -> p (a b c)")
                    nc.vector.scalar_tensor_tensor(sf, sf, KEEP[:, bass.ds(m, 1)], P[:, 4, :],
                                                   ALU.mult, ALU.add).then_inc(state_added, 1)

                def values(it):
                    full(dve, "VP", it)
                    for s in range(SEQ):
                        dst = VP[:, it.par("A"), s].rearrange("p (a b) (q c) -> p a (b q) c", b=2, c=SLOT)
                        ins = nc.vector.tensor_tensor(
                            dst[:, :, 0::3, 0:DH],
                            P[:, BANK["VP"], CH * s:CH * s + CH].rearrange("p (a b d) -> p a b d", b=2, d=DH),
                            BV[:, it.layer("A"), :].rearrange("p (a b d) -> p a b d", b=2, d=DH), ALU.add)
                    ins.then_inc(drained[BANK["VP"]], 1)

                def residual(it, step, other):
                    full(dve, step, it)
                    nc.vector.tensor_tensor(R[:, :, :], P[:, BANK[step], :].rearrange("p (s e) -> p s e", s=SEQ),
                                            other, ALU.add).then_inc(drained[BANK[step]], 1)
                    emptied(dve, step, it)

                def body(it):
                    A, B, C, Dd = (it.active(x) for x in "ABCD")
                    if A:
                        emptied(dve, "XD", it.prev())
                        full(dve, "VP", it.prev())
                        nc.vector.tensor_copy(XS[:, :], XT[:, it.blk("A"), :]).then_inc(xs_ready, 1)
                    if B:
                        mask(it, 0)
                    if C:
                        divide(it, 0)
                        divide(it, 1)
                    if B:
                        mask(it, 1)
                    if C:
                        wait(dve, xk_ready, it.val(1, -1))
                        residual(it, "WO", XK[:, it.blk("C")])
                        statistics(it, 1)
                        normalise(it, 1)
                    if B:
                        mask(it, 2)
                    if A:
                        values(it)
                    if B:
                        add_state(it, 0)
                        mask(it, 3)
                    if C:
                        wait(dve, h1b_ready, it.val(1, 0))
                        residual(it, "W2", H1B[:, :, :])
                        statistics(it, 2)
                    if B:
                        add_state(it, 1)
                    if C:
                        normalise(it, 2)

                pipeline(dve, body)

            @block.gpsimd
            def _(pool):
                def place(dst, src, scale=1.0):
                    return nc.gpsimd.tensor_scalar(dst, src, scale, 0.0, ALU.mult, ALU.add)

                def rstd(it, n):
                    wait(pool, ln_var, it.val(2, n - 2))
                    nc.gpsimd.tensor_tensor(RS[:, :], VE[:, :], NHALF[:, 0:SEQ], ALU.pow).then_inc(ln_rstd, 1)

                def affine(it, n, gain, shift, dst):
                    wait(pool, ln_norm, it.val(2, n - 2))
                    nc.gpsimd.tensor_tensor(N[:, :, :], N[:, :, :], rows(gain, it.layer("C")), ALU.mult) \
                        .then_inc(ln_gain, 1)
                    wait(pool, ln_gain, it.val(2, n - 2))
                    nc.gpsimd.tensor_tensor(dst, N[:, :, :], rows(shift, it.layer("C")), ALU.add) \
                        .then_inc(ln_out, 1)
                    wait(pool, ln_out, it.val(2, n - 2))

                def mask_state(it, j):
                    wait(pool, state_added, it.val(2, 1 + j))
                    wait(pool, keep_ready, it.val(1, 1))
                    nc.gpsimd.tensor_tensor(SK[:, 2 * j:2 * j + 2].rearrange("p a b c -> p (a b) c"),
                                            SF[:, 2 * j:2 * j + 2].rearrange("p a b c -> p (a b) c"),
                                            MK[:, :].unsqueeze(1).to_broadcast([128, 4, 128]),
                                            ALU.mult).then_inc(state_ready, 1)

                def body(it):
                    A, B, C, Dd = (it.active(x) for x in "ABCD")
                    if C:
                        rstd(it, 1)
                        affine(it, 1, G1, BE1, H1[:, :, :])
                        nc.gpsimd.tensor_tensor(H1B[:, :, :], H1[:, :, :], rows(BF2, it.layer("C")), ALU.add) \
                            .then_inc(h1b_ready, 1)
                    if A:
                        emptied(pool, "LK0", it)
                        emptied(pool, "LK1", it)
                        wait(pool, scores_full, it.val(4, 0))
                        nc.gpsimd.tensor_tensor(CARRY[:, 1:2], NHALF[:, 0:1], NHALF[:, 1:2], ALU.mult)
                        for t in range(2):
                            for par in range(2):
                                place(KP[:, it.par("A"), t, par, :], PK[:, t, :], PARM[:, par:par + 1]) \
                                    .then_inc(kp_ready, 1)
                    if B:
                        nc.gpsimd.tensor_tensor(MK[:, :], BDM[:, :],
                                                KEEP[:, bass.ds(it.val(1, 1), 1)].to_broadcast([128, 128]),
                                                ALU.mult).then_inc(keep_ready, 1)
                        mask_state(it, 0)
                    if C:
                        rstd(it, 2)
                    if B:
                        mask_state(it, 1)
                    if C:
                        affine(it, 2, G2, BE2, X2[:, :, :])
                        nc.gpsimd.tensor_tensor(XK[:, it.blk("C")], X2[:, :, :],
                                                rows(BO, it.val(1, -1) // NBLK + 1), ALU.add).then_inc(xk_ready, 1)

                pipeline(pool, body)

        X0 = SM[:, :, :, :, :].rearrange("p a b c d -> p (a b c d)").rearrange("p (n s e) -> p n s e", n=NBLK, s=SEQ)
        X1 = XT[:, :, :].rearrange("p n (s e) -> p n s e", s=SEQ)
        HB = Y[:, :, :].rearrange("p n (s e) -> p n s e", s=SEQ)
        x0_in = sem("x0_in"); o_stats = sem("o_stats"); o_aggr = sem("o_aggr"); o_mv = sem("o_mv"); o_var = sem("o_var")
        o_rstd = sem("o_rstd"); o_norm = sem("o_norm"); x1_ready = sem("x1_ready"); h_ready = sem("h_ready")
        hs_ready = sem("hs_ready"); hb_ready = sem("hb_ready")
        ht_full = sem("ht_full"); ht_copied = sem("ht_copied"); l1_full = sem("l1_full"); l1_added = sem("l1_added")
        gt_full = sem("gt_full"); gelu_done = sem("gelu_done"); l2_full = sem("l2_full"); h_new = sem("h_new")
        q_stats = sem("q_stats"); q_mv = sem("q_mv"); q_var = sem("q_var"); q_rstd = sem("q_rstd")
        q_norm = sem("q_norm"); out_ready = sem("out_ready"); stored = sem("stored")
        STEPS_Q = QBLK * NBLK

        class Q:

            def __init__(self, base, j=0):
                self.base, self.j = base, j

            def val(self, rate, off):
                return self.j * rate + (self.base * rate + off)

        def q_pipeline(eng, body):
            body(Q(0), True, False)
            with eng.Fori(1, STEPS_Q) as j:
                body(Q(0, j), True, True)
            body(Q(STEPS_Q), False, True)

        with nc.Block() as block:
            @block.sync
            def _(sp):
                for s in range(SEQ):
                    sp.dma_start(X0[:, :, s, :], x_dram[s]).then_inc(x0_in, 16)
                for p in range(NBLK):
                    sp.wait_ge(out_ready, p + 1)
                    for s in range(SEQ):
                        sp.dma_start(out_dram[s][:, p, :], XK[:, p, s, :]).then_inc(stored, 16)
                sp.wait_ge(stored, 16 * NBLK * SEQ)

            @block.vector
            def _(dve):
                def all_statistics(src, n):
                    with dve.Fori(0, NBLK) as p:
                        for s in range(SEQ):
                            nc.vector.bn_stats(ST[:, s, :], src[:, p, s, :]).then_inc(o_stats, 1)
                        wait_apart(dve, o_stats, p * SEQ + (n * NBLK * SEQ + SEQ), CARRY[:, 0:1])
                        for s in range(SEQ):
                            nc.vector.bn_aggr(MV[:, s, :], ST[:, s, :]).then_inc(o_aggr, 1)
                        dve.wait_ge(o_aggr, p * SEQ + (n * NBLK * SEQ + SEQ))
                        nc.vector.tensor_copy(MVA[:, p], MV[:, :, :]).then_inc(o_mv, 1)
                    dve.wait_ge(o_mv, (n + 1) * NBLK)
                    nc.vector.tensor_scalar(VEA[:, :], MVA[:, :, :, 1].rearrange("p a b -> p (a b)"), LN_EPS, None,
                                            ALU.add).then_inc(o_var, 1)
                    dve.wait_ge(o_rstd, n + 1)

                def norm_one(dst, src, p):
                    for s in range(SEQ):
                        ins = nc.vector.tensor_scalar(dst[:, s, :], src[:, p, s, :], MVA[:, p, s, 0:1],
                                                      RSA[:, bass.ds(p * SEQ + s, 1)], ALU.subtract, ALU.mult)
                    return ins

                all_statistics(XK, 0)
                dve.wait_ge(x0_in, 64)
                with dve.Fori(0, NBLK) as p:
                    norm_one(N, XK, p).then_inc(o_norm, 1)
                    dve.wait_ge(o_norm, p + 1)
                    nc.vector.tensor_tensor(X1[:, p], N[:, :, :], X0[:, p], ALU.add).then_inc(x1_ready, 1)
                    dve.wait_ge(x1_ready, p + 1)
                all_statistics(X1, 1)
                with dve.Fori(0, NBLK) as p:
                    norm_one(XK[:, p], X1, p).then_inc(h_ready, 1)

                def body(q, first, second):
                    if first:
                        dve.wait_ge(l1_full, q.val(1, 1))
                        nc.vector.tensor_tensor(R[:, :, :], P[:, 2, :].rearrange("p (s e) -> p s e", s=SEQ),
                                                rows(QB, q.val(1, 0) // NBLK * 2), ALU.add).then_inc(l1_added, 1)
                        dve.wait_ge(l1_added, q.val(1, 1))
                        for s in range(SEQ):
                            nc.vector.bn_stats(ST[:, s, :], R[:, s, :]).then_inc(q_stats, 1)
                        wait_apart(dve, q_stats, q.val(4, 4), CARRY[:, 0:1])
                        for s in range(SEQ):
                            nc.vector.bn_aggr(MV[:, s, :], ST[:, s, :]).then_inc(q_mv, 1)
                        dve.wait_ge(q_mv, q.val(4, 4))
                        nc.vector.tensor_scalar(VE[:, :], MV[:, :, 1], LN_EPS, None, ALU.add).then_inc(q_var, 1)
                    if second:
                        dve.wait_ge(l2_full, q.val(1, 0))
                        dve.wait_ge(hb_ready, q.val(1, 0))
                        nc.vector.tensor_tensor(XK[:, (q.val(1, NBLK - 1)) % NBLK],
                                                P[:, 3, :].rearrange("p (s e) -> p s e", s=SEQ), HB[:, q.val(1, 3) % 4],
                                                ALU.add).then_inc(h_new, 1)
                    if first:
                        dve.wait_ge(q_rstd, q.val(1, 1))
                        for s in range(SEQ):
                            ins = nc.vector.tensor_scalar(N[:, s, :], R[:, s, :], MV[:, s, 0:1], RS[:, s:s + 1],
                                                          ALU.subtract, ALU.mult)
                        ins.then_inc(q_norm, 1)

                q_pipeline(dve, body)
                dve.wait_ge(h_new, STEPS_Q)
                all_statistics(XK, 2)
                with dve.Fori(0, NBLK) as p:
                    norm_one(N, XK, p).then_inc(o_norm, 1)
                    dve.wait_ge(o_norm, p + (NBLK + 1))
                    nc.vector.tensor_tensor(XK[:, p], N[:, :, :], X1[:, p], ALU.add).then_inc(out_ready, 1)
                    dve.wait_ge(out_ready, p + 1)

            @block.gpsimd
            def _(pool):
                def all_rstd(n):
                    pool.wait_ge(o_var, n + 1)
                    nc.gpsimd.tensor_tensor(RSA[:, :], VEA[:, :], NHALF[:, :], ALU.pow).then_inc(o_rstd, 1)

                def body(q, first, second):
                    if first:
                        nc.gpsimd.tensor_tensor(X2[:, :, :], XK[:, q.val(1, 0) % NBLK], rows(BO, LAYERS),
                                                ALU.add).then_inc(hs_ready, 1)
                        nc.gpsimd.tensor_tensor(HB[:, q.val(1, 0) % 4], XK[:, q.val(1, 0) % NBLK],
                                                rows(QB, q.val(1, 0) // NBLK * 2 + 1), ALU.add).then_inc(hb_ready, 1)
                        pool.wait_ge(q_var, q.val(1, 1))
                        nc.gpsimd.tensor_tensor(RS[:, :], VE[:, :], NHALF[:, 0:SEQ], ALU.pow).then_inc(q_rstd, 1)

                all_rstd(0)
                all_rstd(1)
                pool.wait_ge(h_ready, NBLK)
                q_pipeline(pool, body)
                all_rstd(2)

            @block.scalar
            def _(act):
                def body(q, first, second):
                    if first:
                        act.wait_ge(ht_full, q.val(1, 1))
                        nc.scalar.activation(HF[:, :], P[:, 0, :], ACT.Copy).then_inc(ht_copied, 1)
                    if second:
                        blk = (q.val(1, -1)) // NBLK
                        act.wait_ge(gt_full, q.val(1, 0))
                        nc.scalar.activation(AF[:, :], P[:, 1, :], ACT.Gelu, bias=QG[:, 1, bass.ds(blk, 1)],
                                             scale=QG[:, 0, bass.ds(blk, 1)]).then_inc(gelu_done, 1)

                q_pipeline(act, body)

            @block.tensor
            def _(pe):
                def body(q, first, second):
                    if first:
                        pe.wait_ge(hs_ready, q.val(1, 1))
                        wait(pe, ht_copied, q.val(1, 0))
                        for s in range(SEQ):
                            ins = nc.tensor.transpose(P[:, 0, CH * s:CH * s + CH], X2[:, s, :], IDN[:, :])
                        ins.then_inc(ht_full, 1)
                    if second:
                        pe.wait_ge(q_norm, q.val(1, 0))
                        for s in range(SEQ):
                            ins = nc.tensor.transpose(P[:, 1, CH * s:CH * s + CH], N[:, s, :], IDN[:, :])
                        ins.then_inc(gt_full, 1)
                    if first:
                        pe.wait_ge(ht_copied, q.val(1, 1))
                        wait(pe, l1_added, q.val(1, 0))
                        for s in range(SEQ):
                            ins = nc.tensor.matmul(P[:, 2, CH * s:CH * s + CH], HF[:, CH * s:CH * s + CH],
                                                   WE[:, (q.val(1, 0)) // NBLK * 2, :], start=True, stop=True)
                        ins.then_inc(l1_full, 1)
                    if second:
                        pe.wait_ge(gelu_done, q.val(1, 0))
                        for s in range(SEQ):
                            ins = nc.tensor.matmul(P[:, 3, CH * s:CH * s + CH], AF[:, CH * s:CH * s + CH],
                                                   WE[:, (q.val(1, -1)) // NBLK * 2 + 1, :], start=True, stop=True)
                        ins.then_inc(l2_full, 1)

                q_pipeline(pe, body)


_INS = ["L0_attn_x", "L0_attn_Wq", "L0_attn_bq", "L0_attn_Wk", "L0_attn_bk", "L0_attn_Wv", "L0_attn_bv",
        "L0_attn_Wo", "L0_attn_bo", "L0_attn_omega", "L0_attn_g1", "L0_attn_be1", "L0_attn_W1", "L0_attn_bf1",
        "L0_attn_W2", "L0_attn_bf2", "L0_attn_g2", "L0_attn_be2", "L0_ffn_qweights", "L0_ffn_scales",
        "L0_ffn_biases", "L0_ffn_lora_a", "L0_ffn_lora_b", "L0_ffn_ln_gamma", "L0_ffn_ln_beta"]
_OUTS = [((4, 1024, 128), "float32")]


def kernel(**inputs):
    import numpy as _np
    import concourse.bacc as _bacc
    from concourse import mybir as _mybir
    from concourse.bass_utils import run_bass_kernel_spmd as _run

    nc = _bacc.Bacc("TRN2", target_bir_lowering=False, num_devices=1)
    arrays, args = {}, []
    for name in _INS:
        a = _np.ascontiguousarray(inputs[name])
        arrays[f"in_{name}_dram"] = a
        args.append(nc.dram_tensor(f"in_{name}_dram", a.shape, _mybir.dt.from_np(a.dtype), kind="ExternalInput").ap())
    for i, (shape, dtype) in enumerate(_OUTS):
        dt = _mybir.dt.from_np(_np.dtype(dtype))
        args.append(nc.dram_tensor(f"out_{i}_dram", shape, dt, kind="ExternalOutput").ap())
    sandwich(nc, *args)
    r = _run(nc, [arrays], core_ids=[0])
    got = tuple(r.results[0][f"out_{i}_dram"] for i in range(len(_OUTS)))
    return got[0]
```

```python
import concourse.bass as bass
from concourse import mybir
from contextlib import ExitStack
import numpy as np

F32 = mybir.dt.float32
F32R = mybir.dt.float32r
I32 = mybir.dt.int32
ACT = mybir.ActivationFunctionType
ALU = mybir.AluOpType

LAYERS, HEADS, D, FF, DH, M2 = 6, 16, 128, 512, 8, 8
SEQ, NBLK, CH = 4, 8, 128
TOK = SEQ * CH
TASKS = LAYERS * NBLK
HT_ = HEADS // 2
SLOT = 16
FT = FF // 128
ALL_CONSTS = 25 + 2 * SEQ * 2
W_DMAS = 16 * (2 + 2 * 4 + 5)
W_LAYER = 16 * (4 + 5)
QBLK = 3
LN_EPS = 1e-5
DEN_EPS = 16 * 1e-6
S_X = float(DH) ** -0.25
DEN = 8

RA = 3 * 128 + 2
RC = FF + FT

STEPS = [("T0", 5, "C"), ("T1", 6, "C"), ("QP", 7, "A"), ("KP", 5, "A"), ("AT", 6, "C"), ("LQ0", 7, "A"),
         ("LQ1", 5, "A"), ("WO", 6, "C"), ("LK0", 7, "A"), ("LK1", 5, "A"), ("VP", 6, "A"), ("HT", 7, "C"),
         ("W1_0", 5, "C"), ("XD", 6, "D"), ("W1_1", 7, "C"), ("W1_2", 5, "C"), ("W1_3", 6, "C"),
         ("W2", 7, "C"), ("KT0", 5, "A"), ("KT1", 6, "A")]
LAG = {"A": 1, "B": 0, "C": -1, "D": -2}
LIMIT = {"A": TASKS, "B": TASKS, "C": TASKS, "D": TASKS - NBLK + 3}
FIRST, LAST = -1, TASKS
LOOP0, LOOPS = 3, (TASKS - 3 - 3) // 2
STEPS_Q = QBLK * NBLK
NORM_IN, NORM_ATTN, NORM_Q, NORM_H = 0, NBLK, 3 * NBLK, 3 * NBLK + STEPS_Q
FRONT = {TASKS - 3: (0, 1), TASKS - 2: (2, 3), TASKS - 1: (4, 5), TASKS: (6,)}
BANK = {s: b for s, b, _ in STEPS}


class It:

    def __init__(self, base, k=None):
        self.base, self.k = base, k

    def val(self, rate, off):
        v = rate * self.base + off
        return v if self.k is None else self.k * (2 * rate) + v

    def active(self, stage):
        return 0 <= self.base + LAG[stage] < LIMIT[stage]

    def par(self, stage):
        return (self.base + LAG[stage]) % 2

    def layer(self, stage):
        b = self.val(1, LAG[stage])
        return b // NBLK

    def blk(self, stage):
        b = self.val(1, LAG[stage])
        return b % NBLK

    def prev(self):
        return It(self.base - 1, self.k)


def fills(step, it):
    bank, n = BANK[step], 0
    for s, b, stage in STEPS:
        if b != bank:
            continue
        upto = it.base if [x[0] for x in STEPS].index(s) <= [x[0] for x in STEPS].index(step) else it.base - 1
        n += max(0, min(upto + LAG[stage], LIMIT[stage] - 1) + 1)
    if it.k is None:
        return n
    assert it.base >= 2
    return it.k * (2 * sum(b == bank for _, b, _ in STEPS)) + n


def wait(eng, sem, value):
    if isinstance(value, int) and value <= 0:
        return
    eng.wait_ge(sem, value)


def norm_number(kind, p):
    if p < 6:
        return NORM_ATTN + 4 * (p // 2) + 2 * (kind - 1) + p % 2
    return NORM_ATTN + (12 if p == 6 else 16) + kind - 1


def norm_of_step(it, back=0):
    if it.k is None and it.base - back < 2:
        return NORM_Q - 2 + it.base - back
    return it.val(1, NORM_Q - back)


def pairs(eng, first, loop_from, loops, last, body):
    for j in range(first, loop_from):
        body(It(j))
    with eng.Fori(0, loops) as k:
        for par in range(2):
            body(It(loop_from + par, k))
    for j in range(loop_from + 2 * loops, last + 1):
        body(It(j))


def wait_apart(eng, sem, value, scratch):
    wait(eng, sem, value)
    eng.memset(scratch, 0.0)


def sandwich(nc, x, Wq, bq, Wk, bk, Wv, bv, Wo, bo, omega, g1, be1, W1, bf1, W2, bf2, g2, be2,
             qw, qscale, qbias, lora_a, lora_b, ln_g, ln_b, out):
    ctx = ExitStack()

    def sb(name, shape, dt=F32):
        return ctx.enter_context(nc.sbuf_tensor(name, shape, dt))

    def sem(name):
        return ctx.enter_context(nc.semaphore(name))

    with ctx:
        XT = sb("x_feat", [128, NBLK, TOK])
        XK = sb("x_tok", [128, NBLK, SEQ, D])
        WA = sb("w_rec_a", [128, LAYERS, RA])
        WC = sb("w_rec_c", [128, LAYERS, RC])
        WV = sb("w_v", [128, LAYERS, D])
        WO = sb("w_o", [128, LAYERS, D])
        WD = sb("w_2", [128, 2, FT, D])
        BV = sb("bv_rows", [128, LAYERS, D])
        BO = sb("bo_rows", [128, LAYERS + 1, D])
        G1 = sb("g1_rows", [128, 2, D])
        BE1 = sb("be1_rows", [128, 2, D])
        BF2 = sb("bf2_rows", [128, 2, D])
        G2 = sb("g2_rows", [128, 2, D])
        BE2 = sb("be2_rows", [128, 2, D])
        WE = sb("w_eff", [128, 2 * QBLK, D])
        QB = sb("q_bias_rows", [128, 2 * QBLK, D])
        QG = sb("q_gamma_beta", [128, 2, QBLK])
        IDN = sb("identity", [128, 128])
        TRI = sb("causal", [128, 128])
        BDM = sb("head_blocks", [128, 128])
        HM8 = sb("head_of_row", [128, HT_])
        PARM = sb("head_parity", [128, 2])
        KEEP = sb("keep_state", [128, TASKS + 1])
        NHALF = sb("minus_half", [128, SEQ])
        CA = sb("cur_a", [128, RA])
        CCH = sb("cur_w1_hi", [128, FF], F32R)
        CCL = sb("cur_w1_lo", [128, FF], F32R)
        CB = sb("cur_bf1", [128, FT])
        XS = sb("x_feat_cur", [128, TOK])
        PQ = sb("phi_q", [128, 2, 2, TOK])
        PK = sb("phi_k", [128, 2, TOK])
        QEH = sb("phi_q_parity_hi", [128, SEQ, 2, 2, CH], F32R)
        QEL = sb("phi_q_parity_lo", [128, SEQ, 2, 2, CH], F32R)
        KH = sb("phi_k_hi", [128, 2, TOK], F32R)
        KL = sb("phi_k_lo", [128, 2, TOK], F32R)
        KTK = sb("phi_k_tok", [128, SEQ, 2, 128])
        VP = sb("v_padded", [128, 2, SEQ, HEADS, 32])
        SM = sb("scores_masked", [128, 2, 4, 4, CH])
        SF = sb("state_full", [128, SEQ, 2, 128])
        SK = sb("state_masked", [128, SEQ, 2, 128])
        MK = sb("keep_blocks", [128, 128])
        OS = sb("attn_num_den", [128, SEQ, 2, CH])
        DN = sb("den", [128, 2, 32])
        AK = sb("attn_tok", [128, SEQ, D])
        AF = sb("attn_feat", [128, TOK])
        R = sb("ln_in", [128, SEQ, D])
        N = sb("ln_out", [128, SEQ, D])
        ST = sb("ln_stats", [128, SEQ, 6])
        MV = sb("ln_mean_var", [128, SEQ, 2])
        VE = sb("ln_var_eps", [128, SEQ])
        RS = sb("ln_rstd", [128, SEQ])
        NM = sb("ln_minus_mean", [128, SEQ])
        SHF = sb("ln_shift", [128, SEQ])
        H1 = sb("h1_tok", [128, SEQ, D])
        H1B = sb("h1_bias_tok", [128, SEQ, D])
        HFH = sb("h1_feat_hi", [128, TOK], F32R)
        HFL = sb("h1_feat_lo", [128, TOK], F32R)
        Y = sb("ff_feat", [128, FT, TOK])
        QS = Y
        X2 = sb("x_tok_cur", [128, SEQ, D])
        CARRY = sb("wait_carrier", [128, 2])
        NMV = sb("norm_mean_var", [128, 2, SEQ, 2])
        NNM = sb("norm_minus_mean", [128, 2, SEQ])
        NVE = sb("norm_var_eps", [128, 2, SEQ])
        NRS = sb("norm_rstd", [128, 2, SEQ])
        NSH = sb("norm_shift", [128, 2, SEQ])
        P = ctx.enter_context(nc.psum_tensor("banks", [128, 8, 512], F32))

        def rows(table, l):
            return table[:, l, :].unsqueeze(1).to_broadcast([128, SEQ, D])

        x_dram = [x[s].rearrange("(p i) f -> i p f", i=CH) for s in range(SEQ)]
        out_dram = [out[s].rearrange("(p i) f -> i p f", i=CH) for s in range(SEQ)]

        x_first = sem("x_first"); x_rest = sem("x_rest")
        om_in = sem("omega_in"); wa_in = sem("w_a_in"); bo_in = sem("bo_in"); wv_in = sem("w_v_in")
        w_in = sem("w_in"); q_tables_in = sem("q_tables_in"); q_in = sem("q_in"); x0_in = sem("x0_in")
        consts = sem("consts"); zeroed = sem("zeroed")
        om_step = sem("om_step"); bias_done = sem("bias_done")
        n_stats = sem("norm_stats_ready")
        n_mv = sem("norm_mean_var_ready")
        n_var = sem("norm_var_ready")
        n_rstd = sem("norm_rstd_ready")
        n_shift = sem("norm_shift_ready")
        n_out = sem("norm_out_ready")
        pre_t = sem("input_transposed"); pre_xt = sem("input_feat_ready"); pre_xk = sem("input_tok_ready")
        dq_step = sem("dequantised"); lb_t = sem("lora_b_transposed"); lb_sb = sem("lora_b_ready")
        we_ps = sem("w_eff_full"); we_sb = sem("w_eff_ready")
        x1_ready = sem("x1_ready")
        h_ready = sem("h_ready")
        hs_ready = sem("h_cur_ready")
        hb_ready = sem("h_bias_ready")
        ht_full = sem("h_feat_full"); ht_copied = sem("h_feat_ready")
        l1_full = sem("first_product_full"); l1_added = sem("first_product_ready")
        gt_full = sem("normed_feat_full"); gelu_done = sem("gelu_ready"); l2_full = sem("second_product_full")
        out_ready = sem("out_ready"); stored = sem("stored")

        OMR = Y[0:64, 0, 0:LAYERS * M2].rearrange("p (l m) -> p l m", l=LAYERS)
        NW = 2 * QBLK
        spare = VP[:, :, :, :, :].rearrange("p a b c d -> p (a b c d)")[:, 4 * TOK:]
        QI = spare[:, 0:NW * D].rearrange("p (w d) -> p w d", w=NW).bitcast(I32)
        QW = spare[:, NW * D:2 * NW * D].rearrange("p (w d) -> p w d", w=NW)
        LA = PK[0:32, :, :].rearrange("p a b -> p (a b)")[:, 0:NW * D].rearrange("p (w d) -> p w d", w=NW)
        LBT = PQ[0:32, 0].rearrange("p a b -> p (a b)")[:, 0:NW * D].rearrange("p (w d) -> p w d", w=NW)
        QSC = XS[:, 0:8 * NW].rearrange("p (w g) -> p w g", w=NW)
        LB = XS[:, 64:64 + 32 * NW].rearrange("p (w r) -> p w r", w=NW)
        XN = (X2, H1)
        X1 = XT[:, :, :].rearrange("p n (s e) -> p n s e", s=SEQ)
        HB = VP[:, 0].rearrange("p a b c -> p (a b c)").rearrange("p (n s e) -> p n s e", n=4, s=SEQ)
        free = SM[:, :, :, :, :].rearrange("p a b c d -> p (a b c d)").rearrange("p (n t) -> p n t", n=8)
        HS = free[:, 0].rearrange("p (s e) -> p s e", s=SEQ)
        RQ = [free[:, 1 + j].rearrange("p (s e) -> p s e", s=SEQ) for j in range(2)]
        NQ = [free[:, 3 + j].rearrange("p (s e) -> p s e", s=SEQ) for j in range(2)]
        HFQ = free[:, 5]
        GF = free[:, 6]

        filled = {b: sem(f"bank{b}_filled") for b in (5, 6, 7)}
        drained = {b: sem(f"bank{b}_drained") for b in (5, 6, 7)}
        scores_full = sem("scores_full")
        scores_masked = sem("scores_masked")
        av_done = sem("av_done")
        o_copied = sem("o_copied")
        state_full = sem("state_full")
        state_added = sem("state_added")
        state_ready = sem("state_ready")
        keep_ready = sem("keep_ready")
        qk_hi = sem("scores_operands_hi")
        qk_lo = sem("scores_operands_lo")
        hf_hi = sem("h1_feat_hi_ready")
        wcl_ready = sem("w1_lo_ready")
        xs_ready = sem("xs_ready")
        wa_ready = sem("wa_ready")
        wc_ready = sem("wc_ready")
        den_step = sem("den_step")
        ln_in = sem("ln_in_ready")
        ln_stats = sem("ln_stats_ready")
        ln_mv = sem("ln_mean_var_ready")
        ln_var = sem("ln_var_eps_ready")
        ln_rstd = sem("ln_rstd_ready")
        ln_nm = sem("ln_minus_mean_ready")
        ln_shift = sem("ln_shift_ready")
        ln_norm1 = sem("ln_norm1_ready")
        ln_norm2 = sem("ln_norm2_ready")
        ln_gain = sem("ln_gain_ready")
        ln_out = sem("ln_out_ready")
        h1b_ready = sem("h1b_ready")
        xk_ready = sem("xk_ready")

        def full(eng, step, it):
            wait(eng, filled[BANK[step]], fills(step, it))

        def layer_loaded(eng, it):
            wait(eng, w_in, it.layer("C") * W_LAYER + (W_DMAS - W_LAYER))

        def emptied(eng, step, it):
            wait(eng, drained[BANK[step]], fills(step, it))

        def claim(eng, step, it):
            n = fills(step, it)
            wait(eng, drained[BANK[step]], n - 1 if isinstance(n, int) else n + -1)

        def pipeline(eng, body):
            pairs(eng, FIRST, LOOP0, LOOPS, LAST, body)

        def v_dense(par, s, t):
            return VP[:, par, s, HT_ * t:HT_ * t + HT_, :].rearrange("p (a b) (q c) -> p a (b q) c", b=2, c=SLOT)[:, :, 0::3, :]

        def bank4(s):
            return P[:, 4, 256 * (s % 2):256 * (s % 2) + 256].rearrange("p (t i) -> p t i", t=2)

        with nc.Block() as block:
            @block.sync
            def _(sp):
                blocks = x.rearrange("s (p i) f -> p i s f", i=CH)
                sp.dma_start(XK[:, 0], blocks[0]).then_inc(x_first, 16)
                for s in range(SEQ):
                    sp.dma_start(XK[:, 1:, s, :], x_dram[s][:, 1:, :]).then_inc(x_rest, 16)
                sp.dma_start(BO[:, 0:LAYERS, :], bo.partition_broadcast(128)).then_inc(bo_in, 16)
                sp.dma_start(WV[:, :, :], Wv.rearrange("l d e -> d l e")).then_inc(wv_in, 16)
                sp.dma_start(BV[:, :, :], bv.partition_broadcast(128)).then_inc(wv_in, 16)
                sp.dma_start(WO[:, :, :], Wo.rearrange("l d e -> d l e")).then_inc(w_in, 16)
                sp.dma_start(WC[:, :, 0:FF], W1.rearrange("l d f -> d l f")).then_inc(w_in, 16)
                with nc.allow_non_contiguous_dma(reason="small tables by feature"):
                    for t in range(FT):
                        sp.dma_start(WC[:, :, FF + t], bf1[:, 128 * t:128 * t + 128].rearrange("l f -> f l")) \
                            .then_inc(w_in, 16)
                for t in range(FT):
                    sp.dma_start(WD[:, :, t, :], W2[0:2, 128 * t:128 * t + 128, :].rearrange("l f d -> f l d")) \
                        .then_inc(w_in, 16)
                for table, src in ((G1, g1), (BE1, be1), (BF2, bf2), (G2, g2), (BE2, be2)):
                    sp.dma_start(table[:, :, :], src[0:2].partition_broadcast(128)).then_inc(w_in, 16)
                sp.dma_start(QB[:, :, :], qbias.partition_broadcast(128)).then_inc(q_tables_in, 16)
                with nc.allow_non_contiguous_dma(reason="small tables by feature"):
                    sp.dma_start(QG[:, 0, :], ln_g.rearrange("l f -> f l")).then_inc(q_tables_in, 16)
                    sp.dma_start(QG[:, 1, :], ln_b.rearrange("l f -> f l")).then_inc(q_tables_in, 16)
                for l in range(2, LAYERS):
                    wait(sp, xk_ready, NBLK * (l - 1) + 1)
                    for t in range(FT):
                        sp.dma_start(WD[:, l % 2, t, :], W2[l, 128 * t:128 * t + 128, :]).then_inc(w_in, 16)
                    for table, src in ((G1, g1), (BE1, be1), (BF2, bf2), (G2, g2), (BE2, be2)):
                        sp.dma_start(table[:, l % 2, :], src[l].partition_broadcast(128)).then_inc(w_in, 16)
                emptied(sp, "XD", It(LOOP0 + 2 * LOOPS - 1))
                for p in range(NBLK):
                    last_read = It(TASKS - NBLK + p - 1)
                    full(sp, "QP", last_read)
                    full(sp, "KP", last_read)
                    wait(sp, xs_ready, TASKS - NBLK + p + 1)
                    wait(sp, x0_in, 16 * p)
                    sp.dma_start(X1[:, p], blocks[p]).then_inc(x0_in, 16)
                wait(sp, av_done, SEQ * TASKS)
                wait(sp, qk_lo, 3 * SEQ * TASKS)
                full(sp, "KT1", It(TASKS - 2))
                full(sp, "VP", It(TASKS - 2))
                sp.dma_start(QI, qw.rearrange("w o d -> o w d")).then_inc(q_in, 16)
                sp.dma_start(QSC, qscale.rearrange("w o g -> o w g")).then_inc(q_in, 16)
                sp.dma_start(LA, lora_a.rearrange("w r d -> r w d")).then_inc(q_in, 16)
                sp.dma_start(LB, lora_b.rearrange("w o r -> o w r")).then_inc(q_in, 16)
                out_blocks = out.rearrange("s (p i) f -> p i s f", i=CH)
                for p in range(NBLK):
                    sp.wait_ge(out_ready, p + 1)
                    sp.dma_start(out_blocks[p], XK[:, p]).then_inc(stored, 16)
                sp.wait_ge(stored, 16 * NBLK)

            @block.tensor
            def _(pe):
                pe.wait_ge(consts, 4)

                def transpose_input(it):
                    wait(pe, n_out, it.val(1, NORM_IN + 1))
                    wait(pe, pre_xt, it.val(1, -1))
                    for s in range(SEQ):
                        ins = nc.tensor.transpose(P[:, it.base % 2, CH * s:CH * s + CH], XN[it.base % 2][:, s, :],
                                                  IDN[:, :])
                    ins.then_inc(pre_t, 1)

                pairs(pe, 0, 2, NBLK // 2 - 1, NBLK - 1, transpose_input)
                pe.wait_ge(pre_xt, NBLK)

                def fill(step, it, ins):
                    ins.then_inc(filled[BANK[step]], 1)

                def scores(it, s, half):
                    if half == 0:
                        wait(pe, qk_lo, it.val(3 * SEQ, 3 * s + 3))
                    for n, (key, query) in enumerate(((KH, QEH), (KH, QEL), (KL, QEH))):
                        for g in range(4):
                            if half == 0 and n == 0:
                                wait(pe, scores_masked, it.val(16, 4 * (s - 1) + g + 1))
                            rg = slice(32 * g, 32 * g + 32)
                            ins = nc.tensor.matmul(P[:, g, 2 * CH * half:2 * CH * half + 2 * CH],
                                                   key[rg, half, CH * s:CH * s + CH],
                                                   query[rg, s, half].rearrange("p a i -> p (a i)"),
                                                   start=(n == 0), stop=(n == 2), skip_group_check=True)
                    if half == 1:
                        ins.then_inc(scores_full, 1)

                def attend(it, s):
                    par = it.par("B")
                    o = bank4(s)
                    if s == 0:
                        emptied(pe, "VP", it.prev())
                        wait(pe, state_ready, it.val(2, 0))
                        wait(pe, state_added, it.val(2, 0))
                    if s == 2 and it.base < TASKS - 1:
                        wait(pe, state_added, it.val(2, 1))
                    if s == 2 and it.base == TASKS - 1:
                        wait(pe, o_copied, it.val(2, 1))
                    for t in range(2):
                        nc.tensor.matmul(o[:, t, :], SK[:, s, t, :], PQ[:, par, t, CH * s:CH * s + CH],
                                         start=(t == 0), stop=False, skip_group_check=True)
                    wait(pe, scores_masked, it.val(16, 4 * s + 4))
                    for sub in range(4):
                        for g in range(4):
                            t, h = sub // 2, 8 * (sub // 2) + 2 * g + sub % 2
                            ins = nc.tensor.matmul(o[32 * g:32 * g + 32, t, :], VP[:, par, s, h, :],
                                                   SM[:, s % 2, g, sub, :], start=False, stop=(sub % 2 == 1),
                                                   skip_group_check=True)
                    ins.then_inc(av_done, 1)

                def state(it, j):
                    par = it.par("B")
                    if j == 0:
                        emptied(pe, "KT1", it.prev())
                    wait(pe, o_copied, it.val(2, 1 + j))
                    for s in (2 * j, 2 * j + 1):
                        for t in range(2):
                            ins = nc.tensor.matmul(bank4(s)[:, t, :], KTK[:, s, t, :], v_dense(par, s, t),
                                                   start=True, stop=True, skip_group_check=True)
                    ins.then_inc(state_full, 1)

                def project(it, step, col):
                    claim(pe, step, it)
                    if step == "QP":
                        wait(pe, wa_ready, it.val(1, 2))
                        emptied(pe, "XD", it.prev())
                    fill(step, it, nc.tensor.matmul(P[:, BANK[step], :], CA[:, col:col + 128],
                                                    XT[:, it.blk("A"), :], start=True, stop=True))

                def logits(it, step, n):
                    claim(pe, step, it)
                    emptied(pe, "QP" if n < 2 else "KP", it)
                    fill(step, it, nc.tensor.matmul(P[:, BANK[step], :], CA[:, 256:384], QS[:, n, :],
                                                    start=True, stop=True))

                def transposes(it, step, srcs):
                    claim(pe, step, it)
                    for n, src in enumerate(srcs):
                        ins = nc.tensor.transpose(P[:, BANK[step], CH * n:CH * n + CH], src, IDN[:, :])
                    fill(step, it, ins)

                def first_product(it, f):
                    step = f"W1_{f}"
                    claim(pe, step, it)
                    for n, (w, h) in enumerate(((CCH, HFH), (CCH, HFL), (CCL, HFH))):
                        ins = nc.tensor.matmul(P[:, BANK[step], :], w[:, 128 * f:128 * f + 128], h[:, :],
                                               start=(n == 0), stop=(n == 2))
                    fill(step, it, ins)

                def lora_b_by_rank():
                    pe.wait_ge(q_in, 64)
                    pe.wait_ge(scores_masked, 16 * TASKS)
                    for w in range(NW):
                        ins = nc.tensor.transpose(P[0:32, w // 4, D * (w % 4):D * (w % 4) + D], LB[:, w, :], IDN[:, :])
                    ins.then_inc(lb_t, 1)

                def effective_weights():
                    pe.wait_ge(dq_step, 2)
                    pe.wait_ge(lb_sb, 2)
                    for w in range(NW):
                        dst = P[:, 2 + w // 4, D * (w % 4):D * (w % 4) + D]
                        nc.tensor.matmul(dst, QW[:, w, :], IDN[:, :], start=True, stop=False)
                        ins = nc.tensor.matmul(dst, LA[:, w, :], LBT[:, w, :], start=False, stop=True)
                    ins.then_inc(we_ps, 1)

                def layers(it):
                    A, B, C, Dd = (it.active(x) for x in "ABCD")
                    if it.base == 0:
                        pe.wait_ge(consts, ALL_CONSTS)
                    if it.base == 1:
                        pe.wait_ge(w_in, W_DMAS)
                    if B:
                        scores(it, 0, 0)
                    if C:
                        for j in range(2):
                            wait(pe, o_copied, it.val(2, j - 1))
                            transposes(it, f"T{j}", [OS[:, s, t, :] for s in (2 * j, 2 * j + 1) for t in range(2)])
                    if it.base == TASKS:
                        lora_b_by_rank()
                    if A:
                        project(it, "QP", 0)
                    if B:
                        scores(it, 0, 1)
                    if A:
                        project(it, "KP", 128)
                    if C:
                        emptied(pe, "T0", it)
                        emptied(pe, "T1", it)
                        transposes(it, "AT", [AK[:, s, :] for s in range(SEQ)])
                    if A:
                        logits(it, "LQ0", 0)
                    if B:
                        scores(it, 1, 0)
                    if A:
                        logits(it, "LQ1", 1)
                    if C:
                        claim(pe, "WO", it)
                        emptied(pe, "AT", it)
                        for s in range(SEQ):
                            ins = nc.tensor.matmul(P[:, BANK["WO"], CH * s:CH * s + CH], AF[:, CH * s:CH * s + CH],
                                                   WO[:, it.layer("C"), :], start=True, stop=True)
                        fill("WO", it, ins)
                    if it.base == TASKS:
                        effective_weights()
                    if B:
                        scores(it, 1, 1)
                    if A:
                        logits(it, "LK0", 2)
                    if B:
                        attend(it, 0)
                    if A:
                        logits(it, "LK1", 3)
                    if B:
                        scores(it, 2, 0)
                    if A:
                        claim(pe, "VP", it)
                        if it.base == FIRST:
                            pe.wait_ge(wv_in, 32)
                        wait(pe, xs_ready, it.val(1, 2))
                        for s in range(SEQ):
                            ins = nc.tensor.matmul(P[:, BANK["VP"], CH * s:CH * s + CH], XS[:, CH * s:CH * s + CH],
                                                   WV[:, it.layer("A"), :], start=True, stop=True)
                        fill("VP", it, ins)
                    if B:
                        scores(it, 2, 1)
                    if C:
                        wait(pe, ln_out, it.val(2, -1))
                        transposes(it, "HT", [H1[:, s, :] for s in range(SEQ)])
                    if B:
                        attend(it, 1)
                    if C:
                        wait(pe, wcl_ready, it.val(1, 0))
                        emptied(pe, "HT", it)
                        first_product(it, 0)
                    if Dd:
                        transposes(it, "XD", [X2[:, s, :] for s in range(SEQ)])
                    if B and it.base < TASKS - 1:
                        state(it, 0)
                    if B:
                        scores(it, 3, 0)
                    if C:
                        first_product(it, 1)
                    if B:
                        scores(it, 3, 1)
                    if C:
                        first_product(it, 2)
                    if B:
                        attend(it, 2)
                    if C:
                        first_product(it, 3)
                    if B:
                        attend(it, 3)
                    if C:
                        claim(pe, "W2", it)
                        layer_loaded(pe, it)
                        emptied(pe, "W1_2", it)
                        emptied(pe, "W1_3", it)
                        for s in range(SEQ):
                            for f in range(FT):
                                ins = nc.tensor.matmul(P[:, BANK["W2"], CH * s:CH * s + CH],
                                                       Y[:, f, CH * s:CH * s + CH], WD[:, it.layer("C") % 2, f, :],
                                                       start=(f == 0), stop=(f == FT - 1))
                        fill("W2", it, ins)
                    if B and it.base < TASKS - 1:
                        state(it, 1)
                    if A:
                        emptied(pe, "LK0", it)
                        for j in range(2):
                            transposes(it, f"KT{j}", [PK[:, t, CH * s:CH * s + CH]
                                                      for s in (2 * j, 2 * j + 1) for t in range(2)])

                pipeline(pe, layers)

                def q_step(it):
                    if 0 <= it.base < STEPS_Q:
                        pe.wait_ge(ht_copied, it.val(1, 1))
                        wait(pe, l1_added, it.val(1, 0))
                        for s in range(SEQ):
                            ins = nc.tensor.matmul(P[:, 2, CH * s:CH * s + CH], HFQ[:, CH * s:CH * s + CH],
                                                   WE[:, it.val(1, 0) // NBLK * 2, :], start=True, stop=True)
                        ins.then_inc(l1_full, 1)
                    if it.base >= 2:
                        pe.wait_ge(n_out, norm_of_step(it, 2) + 1)
                        wait(pe, gelu_done, it.val(1, -2))
                        for s in range(SEQ):
                            ins = nc.tensor.transpose(P[:, 1, CH * s:CH * s + CH], NQ[it.base % 2][:, s, :], IDN[:, :])
                        ins.then_inc(gt_full, 1)
                    if it.base + 1 < STEPS_Q:
                        pe.wait_ge(hs_ready, it.val(1, 2))
                        wait(pe, ht_copied, it.val(1, 1))
                        for s in range(SEQ):
                            ins = nc.tensor.transpose(P[:, 0, CH * s:CH * s + CH], HS[:, s, :], IDN[:, :])
                        ins.then_inc(ht_full, 1)
                    if it.base >= 2:
                        pe.wait_ge(gelu_done, it.val(1, -1))
                        wait(pe, h_ready, it.val(1, NBLK - 2))
                        for s in range(SEQ):
                            ins = nc.tensor.matmul(P[:, 3, CH * s:CH * s + CH], GF[:, CH * s:CH * s + CH],
                                                   WE[:, it.val(1, -2) // NBLK * 2 + 1, :], start=True, stop=True)
                        ins.then_inc(l2_full, 1)

                pe.wait_ge(we_sb, 2)
                pairs(pe, -1, 3, (STEPS_Q - 4) // 2, STEPS_Q + 1, q_step)

            @block.scalar
            def _(act):
                for h in range(HT_):
                    act.dma_start(OMR[8 * h:8 * h + 8], omega.rearrange("l d m -> d l m")).then_inc(om_in, 16)
                act.dma_start(WA[:, :, 0:128], Wq.rearrange("l d e -> d l e")).then_inc(wa_in, 16)
                act.dma_start(WA[:, :, 128:256], Wk.rearrange("l d e -> d l e")).then_inc(wa_in, 16)
                with nc.allow_non_contiguous_dma(reason="small tables by feature"):
                    act.dma_start(WA[:, :, 384], bq.rearrange("l e -> e l")).then_inc(wa_in, 16)
                    act.dma_start(WA[:, :, 385], bk.rearrange("l e -> e l")).then_inc(wa_in, 16)

                def norm(n, par, dst, src):
                    wait(act, n_shift, n + 1)
                    for s in range(SEQ):
                        ins = nc.scalar.activation(dst[:, s, :], src[:, s, :], ACT.Identity,
                                                   bias=NSH[:, par, s:s + 1], scale=NRS[:, par, s:s + 1])
                    ins.then_inc(n_out, 1)

                def norm_input(it):
                    wait(act, pre_t, it.val(1, -1))
                    wait(act, pre_xk, it.val(1, -1))
                    norm(it.val(1, NORM_IN), it.base % 2, XN[it.base % 2], XK[:, it.val(1, 0)])

                pairs(act, 0, 2, NBLK // 2 - 1, NBLK - 1, norm_input)

                def copy_out(it, step, dst, func=ACT.Copy, **kw):
                    full(act, step, it)
                    nc.scalar.activation(dst, P[:, BANK[step], :], func, **kw).then_inc(drained[BANK[step]], 1)

                def front(kind, p):
                    n = norm_number(kind, p)
                    norm(n, n % 2, XK[:, p], XK[:, p] if kind == 1 else X1[:, p])

                def lora_b_by_rank():
                    act.wait_ge(lb_t, 1)
                    for i, ws in enumerate((slice(0, 4), slice(4, NW))):
                        nc.scalar.activation(LBT[:, ws, :].rearrange("p w d -> p (w d)"),
                                             P[0:32, i, 0:D * (ws.stop - ws.start)], ACT.Copy).then_inc(lb_sb, 1)

                def effective_weights():
                    act.wait_ge(we_ps, 1)
                    for i, ws in enumerate((slice(0, 4), slice(4, NW))):
                        nc.scalar.activation(WE[:, ws, :].rearrange("p w d -> p (w d)"),
                                             P[:, 2 + i, 0:D * (ws.stop - ws.start)], ACT.Copy).then_inc(we_sb, 1)

                def lines_squares(it, step, n):
                    full(act, step, it)
                    src, col = P[:, BANK[step], :], 384 + n
                    for half in range(2):
                        hr = slice(64 * half, 64 * half + 64)
                        nc.scalar.activation(QS[0:64, 2 * n + half, :], src[hr, :], ACT.Identity,
                                             bias=CA[hr, col:col + 1], scale=S_X)
                        ins = nc.scalar.activation(QS[64:128, 2 * n + half, :], src[hr, :], ACT.Square,
                                                   bias=CA[hr, col:col + 1], scale=S_X)
                    ins.then_inc(drained[BANK[step]], 1)

                def operands_hi(it, s):
                    wait(act, scores_full, it.val(4, s + 1))
                    i = slice(CH * s, CH * s + CH)
                    for par in range(2):
                        nc.scalar.activation(QEH[:, s, :, par, :], PQ[:, it.par("A"), :, i], ACT.Identity,
                                             scale=PARM[:, par:par + 1]).then_inc(qk_hi, 1)
                    nc.scalar.activation(KH[:, :, i], PK[:, :, i], ACT.Copy).then_inc(qk_hi, 1)

                def attn_copy(it, j):
                    wait(act, av_done, it.val(4, 2 * j + 2))
                    nc.scalar.activation(OS[:, 2 * j:2 * j + 2].rearrange("p a b c -> p (a b c)"), P[:, 4, :],
                                         ACT.Copy).then_inc(o_copied, 1)

                def layers(it):
                    A, B, C, Dd = (it.active(x) for x in "ABCD")
                    if A:
                        lines_squares(it, "QP", 0)
                        lines_squares(it, "KP", 1)
                    if C:
                        copy_out(it, "AT", AF[:, :])
                    if it.base == TASKS:
                        lora_b_by_rank()
                    if A:
                        copy_out(it, "LQ0", PQ[:, it.par("A"), 0, :], ACT.Exp)
                        copy_out(it, "LQ1", PQ[:, it.par("A"), 1, :], ACT.Exp)
                    if C:
                        wait(act, ln_shift, it.val(1, 0))
                        wait(act, ln_out, it.val(2, -2))
                        for s in range(SEQ):
                            ins = nc.scalar.activation(N[:, s, :], R[:, s, :], ACT.Identity, bias=SHF[:, s:s + 1],
                                                       scale=RS[:, s:s + 1])
                        ins.then_inc(ln_norm1, 1)
                    if A:
                        wait(act, qk_lo, it.val(3 * SEQ, 3 * SEQ))
                        copy_out(it, "LK0", PK[:, 0, :], ACT.Exp)
                        copy_out(it, "LK1", PK[:, 1, :], ACT.Exp)
                        if it.base + 2 < TASKS:
                            emptied(act, "KP", it)
                            nc.scalar.activation(CA[:, :], WA[:, it.val(1, 2) // NBLK, :], ACT.Copy) \
                                .then_inc(wa_ready, 1)
                        if it.base == FIRST:
                            act.wait_ge(consts, ALL_CONSTS)
                        emptied(act, "LK0", it)
                        emptied(act, "LK1", it)
                        operands_hi(it, 0)
                        operands_hi(it, 1)
                    if it.base == TASKS:
                        effective_weights()
                    if C:
                        full(act, "HT", it)
                        nc.scalar.activation(HFH[:, :], P[:, BANK["HT"], :], ACT.Copy).then_inc(hf_hi, 1)
                    if B:
                        attn_copy(it, 0)
                    if C:
                        copy_out(it, "W1_0", Y[:, 0, :], ACT.Relu, bias=CB[:, 0:1])
                    if Dd:
                        copy_out(it, "XD", XT[:, it.blk("D"), :])
                    if A:
                        operands_hi(it, 2)
                    if C:
                        for f in range(1, FT):
                            copy_out(it, f"W1_{f}", Y[:, f, :], ACT.Relu, bias=CB[:, f:f + 1])
                    if B:
                        if it.base == 0:
                            act.wait_ge(w_in, W_DMAS)
                        emptied(act, "W1_2", it)
                        emptied(act, "W1_3", it)
                        l = it.val(1, 0) // NBLK
                        nc.scalar.activation(CCH[:, :], WC[:, l, 0:FF], ACT.Copy).then_inc(wc_ready, 1)
                        nc.scalar.activation(CB[:, :], WC[:, l, FF:RC], ACT.Copy).then_inc(wc_ready, 1)
                        attn_copy(it, 1)
                    if A:
                        operands_hi(it, 3)
                    for kind, m in ((2, it.base - 1), (1, it.base)):
                        for p in FRONT.get(m, ()):
                            front(kind, p)
                    if A:
                        for j in range(2):
                            copy_out(it, f"KT{j}", KTK[:, 2 * j:2 * j + 2].rearrange("p a b c -> p (a b c)"))


                act.wait_ge(om_step, 3)
                act.wait_ge(bias_done, 1)
                nc.scalar.activation(CA[:, :], WA[:, 0, :], ACT.Copy).then_inc(wa_ready, 1)
                pipeline(act, layers)

                def norm_step(it, back):
                    par = (it.base - back) % 2
                    wait(act, gt_full, it.val(1, -back - 1))
                    norm(norm_of_step(it, back), par, NQ[par], RQ[par])

                def q_step(it):
                    if it.base >= 2:
                        blk = it.val(1, -2) // NBLK
                        act.wait_ge(gt_full, it.val(1, -1))
                        wait(act, l2_full, it.val(1, -2))
                        nc.scalar.activation(GF[:, :], P[:, 1, :], ACT.Gelu, bias=QG[:, 1, bass.ds(blk, 1)],
                                             scale=QG[:, 0, bass.ds(blk, 1)]).then_inc(gelu_done, 1)
                    if it.base + 1 < STEPS_Q:
                        act.wait_ge(ht_full, it.val(1, 2))
                        wait(act, l1_full, it.val(1, 1))
                        nc.scalar.activation(HFQ[:, :], P[:, 0, :], ACT.Copy).then_inc(ht_copied, 1)
                    if 3 <= it.base <= STEPS_Q:
                        norm_step(it, 1)

                def norm_h(it):
                    h = XK[:, it.val(1, 0)]
                    norm(it.val(1, NORM_H), it.base % 2, h, h)

                front(2, 6)
                act.wait_ge(av_done, SEQ * TASKS)
                act.wait_ge(q_tables_in, 48)
                nc.scalar.activation(CARRY[:, 1:2], QG[:, 0, 0:1], ACT.Gelu)
                q_step(It(-1))
                for j in (0, 1):
                    q_step(It(j))
                    norm_step(It(j), 0)
                front(1, 7)
                front(2, 7)
                pairs(act, 2, 3, (STEPS_Q - 4) // 2, STEPS_Q + 1, q_step)
                pairs(act, 0, 2, NBLK // 2 - 1, NBLK - 1, norm_h)

            @block.vector
            def _(dve):
                nc.vector.memset(VP[:, :, :, :, :], 0.0).then_inc(zeroed, 1)
                nc.vector.memset(SK[:, :, :, :], 0.0).then_inc(zeroed, 1)
                nc.vector.memset(SF[:, :, :, :], 0.0).then_inc(zeroed, 1)

                def norm_statistics(n, par, src):
                    for s in range(SEQ):
                        nc.vector.bn_stats(ST[:, s, :], src[:, s, :]).then_inc(n_stats, 1)
                    wait(dve, n_var, 2 * n - 2 if isinstance(n, int) else 2 * n + -2)
                    wait_apart(dve, n_stats, 4 * n + 4, CARRY[:, 0:1])
                    for s in range(SEQ):
                        nc.vector.bn_aggr(NMV[:, par, s, :], ST[:, s, :]).then_inc(n_mv, 1)
                    wait(dve, n_mv, 4 * n + 4)
                    wait(dve, n_shift, n - 1 if isinstance(n, int) else n + -1)
                    nc.vector.tensor_scalar(NNM[:, par, :], NMV[:, par, :, 0], -1.0, None, ALU.mult).then_inc(n_var, 1)
                    nc.vector.tensor_scalar(NVE[:, par, :], NMV[:, par, :, 1], LN_EPS, None, ALU.add).then_inc(n_var, 1)

                def input_block(it):
                    if it.base < NBLK:
                        norm_statistics(it.val(1, NORM_IN), it.base % 2, XK[:, it.val(1, 0)])
                    if it.base >= 2:
                        wait(dve, pre_t, it.val(1, -1))
                        nc.vector.tensor_copy(XT[:, it.val(1, -2), :], P[:, it.base % 2, :]).then_inc(pre_xt, 1)

                dve.wait_ge(x_first, 16)
                input_block(It(0))
                dve.wait_ge(x_rest, 16 * SEQ)
                input_block(It(1))
                dve.wait_ge(om_in, 16 * HT_)
                dve.wait_ge(consts, 8)
                om = WA[:, :, 256:384].rearrange("p l (h g m) -> p l h g m", h=HT_, g=2)
                nc.vector.tensor_tensor(om[0:64, :, :, 0, :],
                                        OMR[:, :, :].unsqueeze(2).to_broadcast([64, LAYERS, HT_, M2]),
                                        HM8[0:64, :].unsqueeze(1).unsqueeze(3).to_broadcast([64, LAYERS, HT_, M2]),
                                        ALU.mult).then_inc(om_step, 1)
                dve.wait_ge(om_step, 1)
                nc.vector.tensor_scalar(om[0:64, :, :, 1, :], om[0:64, :, :, 0, :], -1.0, None, ALU.mult) \
                    .then_inc(om_step, 1)
                nc.vector.tensor_scalar(WA[64:128, :, 256:384].rearrange("p l (h c) -> p l h c", h=HT_),
                                        HM8[64:128, :].unsqueeze(1).unsqueeze(3)
                                        .to_broadcast([64, LAYERS, HT_, 2 * M2]),
                                        -0.5, None, ALU.mult).then_inc(om_step, 1)

                pairs(dve, 2, 2, NBLK // 2 - 1, NBLK + 1, input_block)
                dve.wait_ge(wa_in, 64)
                nc.vector.tensor_scalar(WA[:, :, 384:386], WA[:, :, 384:386], S_X, None, ALU.mult) \
                    .then_inc(bias_done, 1)
                dve.wait_ge(pre_xt, NBLK)
                dve.wait_ge(pre_xk, NBLK)
                dve.wait_ge(consts, ALL_CONSTS)

                def mask(it, s):
                    wait(dve, scores_full, it.val(4, s + 1))
                    wait(dve, av_done, it.val(4, s - 1))
                    for g in range(4):
                        nc.vector.tensor_tensor(SM[:, s % 2, g, :, :], P[:, g, :].rearrange("p (a i) -> p a i", a=4),
                                                TRI[:, :].unsqueeze(1).to_broadcast([128, 4, 128]),
                                                ALU.mult).then_inc(scores_masked, 1)

                def divide(it, j):
                    full(dve, f"T{j}", it)
                    t = P[:, BANK[f"T{j}"], :].rearrange("p (h c) -> p h c", c=SLOT)
                    nc.vector.tensor_scalar(DN[:, 0, :], t[:, :, DEN], DEN_EPS, None, ALU.add).then_inc(den_step, 1)
                    wait(dve, den_step, it.val(4, 2 * j - 3))
                    nc.vector.reciprocal(DN[:, 1, :], DN[:, 0, :]).then_inc(den_step, 1)
                    wait(dve, den_step, it.val(4, 2 * j - 2))
                    nc.vector.tensor_tensor(AK[:, 2 * j:2 * j + 2, :].rearrange("p s (h d) -> p (s h) d", d=DH),
                                            t[:, :, 0:DH], DN[:, 1, :].unsqueeze(2).to_broadcast([128, 32, DH]),
                                            ALU.mult).then_inc(drained[BANK[f"T{j}"]], 1)

                def statistics(it, n):
                    for s in range(SEQ):
                        nc.vector.bn_stats(ST[:, s, :], R[:, s, :]).then_inc(ln_stats, 1)
                    wait_apart(dve, ln_stats, it.val(8, 4 * n - 8), CARRY[:, 0:1])
                    for s in range(SEQ):
                        nc.vector.bn_aggr(MV[:, s, :], ST[:, s, :]).then_inc(ln_mv, 1)
                    wait(dve, ln_mv, it.val(8, 4 * n - 8))
                    nc.vector.tensor_scalar(VE[:, :], MV[:, :, 1], LN_EPS, None, ALU.add).then_inc(ln_var, 1)
                    if n == 1:
                        wait(dve, ln_shift, it.val(1, -1))
                        nc.vector.tensor_scalar(NM[:, :], MV[:, :, 0], -1.0, None, ALU.mult).then_inc(ln_nm, 1)

                def normalise(it):
                    wait(dve, ln_rstd, it.val(2, 0))
                    wait(dve, ln_out, it.val(2, -1))
                    for s in range(SEQ):
                        ins = nc.vector.tensor_scalar(N[:, s, :], R[:, s, :], MV[:, s, 0:1], RS[:, s:s + 1],
                                                      ALU.subtract, ALU.mult)
                    ins.then_inc(ln_norm2, 1)

                def operands_lo(it, s):
                    wait(dve, qk_hi, it.val(3 * SEQ, 3 * SEQ + 3 * s + 3))
                    i = slice(CH * s, CH * s + CH)
                    for par in range(2):
                        nc.vector.scalar_tensor_tensor(QEL[:, s, :, par, :], PQ[:, it.par("A"), :, i],
                                                       PARM[:, par:par + 1], QEH[:, s, :, par, :].bitcast(F32),
                                                       ALU.mult, ALU.subtract).then_inc(qk_lo, 1)
                    nc.vector.tensor_tensor(KL[:, :, i], PK[:, :, i], KH[:, :, i].bitcast(F32), ALU.subtract) \
                        .then_inc(qk_lo, 1)

                def add_state(it, j):
                    wait(dve, state_full, it.val(2, 1 + j))
                    wait(dve, state_ready, it.val(2, j - 1))
                    m = it.val(1, 0)
                    sf = SF[:, 2 * j:2 * j + 2].rearrange("p a b c -> p (a b c)")
                    nc.vector.scalar_tensor_tensor(sf, sf, KEEP[:, bass.ds(m, 1)], P[:, 4, :],
                                                   ALU.mult, ALU.add).then_inc(state_added, 1)

                def values(it):
                    full(dve, "VP", it)
                    for s in range(SEQ):
                        dst = VP[:, it.par("A"), s].rearrange("p (a b) (q c) -> p a (b q) c", b=2, c=SLOT)
                        ins = nc.vector.tensor_tensor(
                            dst[:, :, 0::3, 0:DH],
                            P[:, BANK["VP"], CH * s:CH * s + CH].rearrange("p (a b d) -> p a b d", b=2, d=DH),
                            BV[:, it.layer("A"), :].rearrange("p (a b d) -> p a b d", b=2, d=DH), ALU.add)
                    ins.then_inc(drained[BANK["VP"]], 1)

                def residual(it, step, other):
                    full(dve, step, it)
                    nc.vector.tensor_tensor(R[:, :, :], P[:, BANK[step], :].rearrange("p (s e) -> p s e", s=SEQ),
                                            other, ALU.add).then_inc(drained[BANK[step]], 1)
                    emptied(dve, step, it)

                def front(kind, p):
                    n = norm_number(kind, p)
                    if kind == 1:
                        dve.wait_ge(xk_ready, TASKS - NBLK + p + 1)
                        norm_statistics(n, n % 2, XK[:, p])
                    else:
                        dve.wait_ge(n_out, norm_number(1, p) + 1)
                        dve.wait_ge(x0_in, 16 * (p + 1))
                        nc.vector.tensor_tensor(X1[:, p], X1[:, p], XK[:, p], ALU.add).then_inc(x1_ready, 1)
                        dve.wait_ge(x1_ready, p + 1)
                        norm_statistics(n, n % 2, X1[:, p])

                def dequantise():
                    dve.wait_ge(q_in, 64)
                    nc.vector.tensor_scalar(QW, QI, 1.0 / 7.5, -1.0, ALU.mult, ALU.add).then_inc(dq_step, 1)
                    dve.wait_ge(dq_step, 1)
                    v = QW.rearrange("p w (g c) -> p w g c", c=16)
                    nc.vector.tensor_tensor(v, v, QSC.unsqueeze(3).to_broadcast([128, NW, 8, 16]), ALU.mult) \
                        .then_inc(dq_step, 1)

                def layers(it):
                    A, B, C, Dd = (it.active(x) for x in "ABCD")
                    if A:
                        emptied(dve, "XD", it.prev())
                        full(dve, "VP", it.prev())
                        nc.vector.tensor_copy(XS[:, :], XT[:, it.blk("A"), :]).then_inc(xs_ready, 1)
                    if C:
                        divide(it, 0)
                        divide(it, 1)
                    if B:
                        mask(it, 0)
                    if C:
                        wait(dve, xk_ready, it.val(1, -1))
                        residual(it, "WO", XK[:, it.blk("C")])
                        statistics(it, 1)
                        if it.base == TASKS:
                            dequantise()
                    if B:
                        mask(it, 1)
                    for kind, m in ((2, it.base - 1), (1, it.base)):
                        for p in FRONT.get(m, ()):
                            front(kind, p)
                    if A:
                        if it.base == FIRST:
                            dve.wait_ge(wv_in, 32)
                        values(it)
                    if C:
                        full(dve, "HT", it)
                        wait(dve, hf_hi, it.val(1, 0))
                        nc.vector.tensor_tensor(HFL[:, :], P[:, BANK["HT"], :], HFH[:, :].bitcast(F32),
                                                ALU.subtract).then_inc(drained[BANK["HT"]], 1)
                    if B:
                        mask(it, 2)
                    if B and it.base < TASKS - 1:
                        add_state(it, 0)
                    if A:
                        operands_lo(it, 0)
                        operands_lo(it, 1)
                    if B:
                        mask(it, 3)
                    if A:
                        operands_lo(it, 2)
                        operands_lo(it, 3)
                    if C:
                        wait(dve, h1b_ready, it.val(1, 0))
                        residual(it, "W2", H1B[:, :, :])
                        statistics(it, 2)
                    if B and it.base < TASKS - 1:
                        add_state(it, 1)
                    if it.base == TASKS:
                        front(2, 6)
                    if C:
                        normalise(it)


                pipeline(dve, layers)

                def q_step(it):
                    if it.base + 1 < STEPS_Q:
                        wait(dve, h_ready, it.val(1, 2))
                        wait(dve, ht_full, it.val(1, 1))
                        nc.vector.tensor_copy(HS[:, :, :], XK[:, it.val(1, 1 + NBLK) % NBLK]).then_inc(hs_ready, 1)
                    if 0 <= it.base < STEPS_Q:
                        wait(dve, l1_full, it.val(1, 1))
                        if it.base >= 2:
                            wait(dve, n_out, norm_of_step(it, 2) + 1)
                        r = RQ[it.base % 2]
                        nc.vector.tensor_tensor(r[:, :, :], P[:, 2, :].rearrange("p (s e) -> p s e", s=SEQ),
                                                rows(QB, it.val(1, 0) // NBLK * 2), ALU.add).then_inc(l1_added, 1)
                        wait(dve, l1_added, it.val(1, 1))
                        norm_statistics(norm_of_step(it), it.base % 2, r)
                    if it.base == 2:
                        dve.wait_ge(n_out, norm_number(2, 7) + 1)
                        dve.memset(CARRY[:, 0:1], 0.0).then_inc(h_ready, 1)
                    if it.base >= 2:
                        wait(dve, l2_full, it.val(1, -1))
                        wait(dve, hb_ready, it.val(1, -1))
                        nc.vector.tensor_tensor(XK[:, it.val(1, NBLK - 2) % NBLK],
                                                P[:, 3, :].rearrange("p (s e) -> p s e", s=SEQ),
                                                HB[:, it.val(1, 2) % 4], ALU.add).then_inc(h_ready, 1)

                def add_x1(it):
                    if it.base < NBLK:
                        wait(dve, h_ready, it.val(1, STEPS_Q + 1))
                        norm_statistics(it.val(1, NORM_H), it.base % 2, XK[:, it.val(1, 0)])
                    if it.base >= 1:
                        wait(dve, n_out, it.val(1, NORM_H))
                        nc.vector.tensor_tensor(XK[:, it.val(1, -1)], XK[:, it.val(1, -1)], X1[:, it.val(1, -1)],
                                                ALU.add).then_inc(out_ready, 1)

                dve.wait_ge(q_tables_in, 48)
                dve.wait_ge(av_done, SEQ * TASKS)
                dve.wait_ge(n_out, norm_number(2, 6) + 1)
                dve.memset(CARRY[:, 0:1], 0.0).then_inc(h_ready, NBLK - 1)
                for j in (-1, 0, 1):
                    q_step(It(j))
                front(1, 7)
                front(2, 7)
                pairs(dve, 2, 3, (STEPS_Q - 4) // 2, STEPS_Q + 1, q_step)
                pairs(dve, 0, 2, NBLK // 2 - 1, NBLK, add_x1)

            @block.gpsimd
            def _(pool):
                def select(t, op, pattern, base, mult, fill, n):
                    pool.wait_ge(consts, n)
                    pool.affine_select(out=t, in_=t, compare_op=op, fill=fill, base=base, pattern=pattern,
                                       channel_multiplier=mult).then_inc(consts, 1)

                def norm_factors(n, par):
                    wait(pool, n_var, 2 * n + 2)
                    wait(pool, n_out, n - 1 if isinstance(n, int) else n + -1)
                    nc.gpsimd.tensor_tensor(NRS[:, par, :], NVE[:, par, :], NHALF[:, :], ALU.pow).then_inc(n_rstd, 1)
                    wait(pool, n_rstd, n + 1)
                    nc.gpsimd.tensor_tensor(NSH[:, par, :], NNM[:, par, :], NRS[:, par, :], ALU.mult) \
                        .then_inc(n_shift, 1)

                pool.memset(IDN[:, :], 0.0).then_inc(consts, 1)
                pool.memset(HM8[:, :], 1.0).then_inc(consts, 1)
                pool.memset(NHALF[:, :], -0.5).then_inc(consts, 1)
                select(IDN[:, :], ALU.not_equal, [[-1, 128]], 0, 1, 1.0, 3)
                for half in range(2):
                    hm = HM8[64 * half:64 * half + 64, :]
                    select(hm, ALU.is_ge, [[-DH, HT_]], 0, 1, 0.0, 4 + 2 * half)
                    select(hm, ALU.is_ge, [[DH, HT_]], DH - 1, -1, 0.0, 5 + 2 * half)

                def input_block(it):
                    if it.base < NBLK:
                        norm_factors(it.val(1, NORM_IN), it.base % 2)
                    if it.base >= 1:
                        wait(pool, n_out, it.val(1, NORM_IN))
                        nc.gpsimd.tensor_tensor(XK[:, it.val(1, -1)], XN[(it.base - 1) % 2][:, :, :], rows(BO, 0),
                                                ALU.add).then_inc(pre_xk, 1)

                pool.wait_ge(consts, 8)
                pool.wait_ge(bo_in, 16)
                pairs(pool, 0, 2, NBLK // 2 - 1, NBLK, input_block)

                pool.memset(TRI[:, :], 1.0).then_inc(consts, 1)
                pool.memset(BDM[:, :], 1.0).then_inc(consts, 1)
                pool.memset(PARM[:, :], 0.0).then_inc(consts, 1)
                pool.memset(KEEP[:, :], 1.0).then_inc(consts, 1)
                bdm = BDM[:, :].rearrange("p (h c) -> p h c", h=HT_)
                select(bdm, ALU.is_ge, [[-SLOT, HT_], [0, SLOT]], 0, 1, 0.0, 12)
                select(bdm, ALU.is_ge, [[SLOT, HT_], [0, SLOT]], SLOT - 1, -1, 0.0, 13)
                for g in range(4):
                    for par in range(2):
                        h = 2 * g + par
                        pool.wait_ge(consts, 14 + 2 * g)
                        pool.tensor_tensor(PARM[:, par:par + 1], PARM[:, par:par + 1],
                                           BDM[:, SLOT * h:SLOT * h + 1], ALU.add).then_inc(consts, 1)
                select(TRI[:, :], ALU.is_ge, [[1, 128]], 0, -1, 0.0, 22)
                pool.memset(KEEP[:, 0:TASKS + 1:NBLK], 0.0).then_inc(consts, 1)
                pool.memset(BO[:, LAYERS, :], 0.0).then_inc(consts, 1)
                pool.wait_ge(zeroed, 3)
                for buf in range(2):
                    for s in range(SEQ):
                        for par in range(2):
                            ones = VP[:, buf, s, par::2, SLOT * par + DEN]
                            pool.memset(ones, 1.0).then_inc(consts, 1)
                pool.wait_ge(consts, ALL_CONSTS)

                def rstd(it, n):
                    wait(pool, ln_var, it.val(2, n - 2))
                    nc.gpsimd.tensor_tensor(RS[:, :], VE[:, :], NHALF[:, 0:SEQ], ALU.pow).then_inc(ln_rstd, 1)

                def affine(it, n, gain, shift, dst):
                    wait(pool, (ln_norm1, ln_norm2)[n - 1], it.val(1, 0))
                    nc.gpsimd.tensor_tensor(N[:, :, :], N[:, :, :], rows(gain, it.layer("C") % 2), ALU.mult) \
                        .then_inc(ln_gain, 1)
                    wait(pool, ln_gain, it.val(2, n - 2))
                    nc.gpsimd.tensor_tensor(dst, N[:, :, :], rows(shift, it.layer("C") % 2), ALU.add) \
                        .then_inc(ln_out, 1)
                    wait(pool, ln_out, it.val(2, n - 2))

                def mask_state(it, j):
                    wait(pool, state_added, it.val(2, 1 + j))
                    wait(pool, keep_ready, it.val(1, 1))
                    nc.gpsimd.tensor_tensor(SK[:, 2 * j:2 * j + 2].rearrange("p a b c -> p (a b) c"),
                                            SF[:, 2 * j:2 * j + 2].rearrange("p a b c -> p (a b) c"),
                                            MK[:, :].unsqueeze(1).to_broadcast([128, 4, 128]),
                                            ALU.mult).then_inc(state_ready, 1)

                def layers(it):
                    A, B, C, Dd = (it.active(x) for x in "ABCD")
                    if it.base == 1:
                        pool.wait_ge(w_in, W_DMAS)
                    if C:
                        layer_loaded(pool, it)
                        rstd(it, 1)
                        wait(pool, ln_nm, it.val(1, 0))
                        wait(pool, ln_norm1, it.val(1, -1))
                        wait(pool, ln_rstd, it.val(2, -1))
                        nc.gpsimd.tensor_tensor(SHF[:, :], NM[:, :], RS[:, :], ALU.mult).then_inc(ln_shift, 1)
                        affine(it, 1, G1, BE1, H1[:, :, :])
                        nc.gpsimd.tensor_tensor(H1B[:, :, :], H1[:, :, :], rows(BF2, it.layer("C") % 2), ALU.add) \
                            .then_inc(h1b_ready, 1)
                    for kind, m in ((2, it.base - 1), (1, it.base)):
                        for p in FRONT.get(m, ()):
                            norm_factors(norm_number(kind, p), norm_number(kind, p) % 2)
                    if B and it.base < TASKS - 1:
                        nc.gpsimd.tensor_tensor(MK[:, :], BDM[:, :],
                                                KEEP[:, bass.ds(it.val(1, 1), 1)].to_broadcast([128, 128]),
                                                ALU.mult).then_inc(keep_ready, 1)
                        mask_state(it, 0)
                    if C:
                        rstd(it, 2)
                    if B and it.base < TASKS - 1:
                        mask_state(it, 1)
                    if it.base == TASKS:
                        norm_factors(norm_number(2, 6), norm_number(2, 6) % 2)
                    if C:
                        affine(it, 2, G2, BE2, X2[:, :, :])
                        nc.gpsimd.tensor_tensor(XK[:, it.blk("C")], X2[:, :, :],
                                                rows(BO, it.val(1, -1) // NBLK + 1), ALU.add).then_inc(xk_ready, 1)
                    if B:
                        wait(pool, wc_ready, it.val(2, 2))
                        nc.gpsimd.tensor_tensor(CCL[:, :], WC[:, it.val(1, 0) // NBLK, 0:FF], CCH[:, :].bitcast(F32),
                                                ALU.subtract).then_inc(wcl_ready, 1)


                pipeline(pool, layers)

                def q_step(it):
                    wait(pool, h_ready, it.val(1, 5) if it.base >= 2 else it.base + 1)
                    nc.gpsimd.tensor_tensor(HB[:, it.val(1, 0) % 4], XK[:, it.val(1, 0) % NBLK],
                                            rows(QB, it.val(1, 0) // NBLK * 2 + 1), ALU.add).then_inc(hb_ready, 1)
                    norm_factors(norm_of_step(it), it.base % 2)

                def factors_h(it):
                    norm_factors(it.val(1, NORM_H), it.base % 2)

                pool.wait_ge(q_tables_in, 48)
                pool.wait_ge(av_done, SEQ * TASKS)
                q_step(It(0))
                q_step(It(1))
                norm_factors(norm_number(1, 7), norm_number(1, 7) % 2)
                norm_factors(norm_number(2, 7), norm_number(2, 7) % 2)
                pairs(pool, 2, 2, (STEPS_Q - 4) // 2, STEPS_Q - 1, q_step)
                pairs(pool, 0, 2, NBLK // 2 - 1, NBLK - 1, factors_h)



_INS = ["L0_attn_x", "L0_attn_Wq", "L0_attn_bq", "L0_attn_Wk", "L0_attn_bk", "L0_attn_Wv", "L0_attn_bv",
        "L0_attn_Wo", "L0_attn_bo", "L0_attn_omega", "L0_attn_g1", "L0_attn_be1", "L0_attn_W1", "L0_attn_bf1",
        "L0_attn_W2", "L0_attn_bf2", "L0_attn_g2", "L0_attn_be2", "L0_ffn_qweights", "L0_ffn_scales",
        "L0_ffn_biases", "L0_ffn_lora_a", "L0_ffn_lora_b", "L0_ffn_ln_gamma", "L0_ffn_ln_beta"]
_OUTS = [((4, 1024, 128), "float32")]


def kernel(**inputs):
    import numpy as _np
    import concourse.bacc as _bacc
    from concourse import mybir as _mybir
    from concourse.bass_utils import run_bass_kernel_spmd as _run

    nc = _bacc.Bacc("TRN2", target_bir_lowering=False, num_devices=1)
    arrays, args = {}, []
    for name in _INS:
        a = _np.ascontiguousarray(inputs[name])
        arrays[f"in_{name}_dram"] = a
        args.append(nc.dram_tensor(f"in_{name}_dram", a.shape, _mybir.dt.from_np(a.dtype), kind="ExternalInput").ap())
    for i, (shape, dtype) in enumerate(_OUTS):
        dt = _mybir.dt.from_np(_np.dtype(dtype))
        args.append(nc.dram_tensor(f"out_{i}_dram", shape, dt, kind="ExternalOutput").ap())
    sandwich(nc, *args)
    r = _run(nc, [arrays], core_ids=[0])
    got = tuple(r.results[0][f"out_{i}_dram"] for i in range(len(_OUTS)))
    return got[0]
```

```python
import concourse.bass as bass
from concourse import mybir
from contextlib import ExitStack
import numpy as np

F32 = mybir.dt.float32
F32R = mybir.dt.float32r
I32 = mybir.dt.int32
ACT = mybir.ActivationFunctionType
ALU = mybir.AluOpType

LAYERS, HEADS, D, FF, DH, M2 = 6, 16, 128, 512, 8, 8
SEQ, NBLK, CH = 4, 8, 128
TOK = SEQ * CH
TASKS = LAYERS * NBLK
HT_ = HEADS // 2
SLOT = 16
FT = FF // 128
ALL_CONSTS = 25 + 2 * SEQ * 2
W_DMAS = 16 * (2 + 2 * 4 + 5)
W_LAYER = 16 * (4 + 5)
QBLK = 3
LN_EPS = 1e-5
DEN_EPS = 16 * 1e-6
S_X = float(DH) ** -0.25
DEN = 8

RA = 3 * 128 + 2
RC = FF + FT

STEPS = [("T0", 5, "C"), ("T1", 6, "C"), ("QP", 7, "A"), ("KP", 5, "A"), ("AT", 6, "C"), ("LQ0", 7, "A"),
         ("LQ1", 6, "A"), ("WO", 5, "C"), ("LK0", 7, "A"), ("LK1", 6, "A"), ("VP", 5, "A"), ("HT", 7, "C"),
         ("XD", 6, "D"), ("W1_0", 5, "C"), ("W1_1", 7, "C"), ("W1_2", 6, "C"), ("W1_3", 5, "C"),
         ("W2", 7, "C"), ("KT0", 5, "A"), ("KT1", 6, "A")]
LAG = {"A": 1, "B": 0, "C": -1, "D": -2}
LIMIT = {"A": TASKS, "B": TASKS, "C": TASKS, "D": TASKS - NBLK + 3}
FIRST, LAST = -1, TASKS
LOOP0, LOOPS = 3, (TASKS - 3 - 3) // 2
STEPS_Q = QBLK * NBLK
STEADY_Q = 6, (STEPS_Q - 8) // 2
NORM_IN, NORM_ATTN, NORM_Q, NORM_H = 0, NBLK, 3 * NBLK, 3 * NBLK + STEPS_Q
FRONT = {TASKS - 3: (0, 1), TASKS - 2: (2, 3), TASKS - 1: (4, 5), TASKS: (6,)}
BANK = {s: b for s, b, _ in STEPS}


class It:

    def __init__(self, base, k=None):
        self.base, self.k = base, k

    def val(self, rate, off):
        v = rate * self.base + off
        return v if self.k is None else self.k * (2 * rate) + v

    def active(self, stage):
        return 0 <= self.base + LAG[stage] < LIMIT[stage]

    def par(self, stage):
        return (self.base + LAG[stage]) % 2

    def layer(self, stage):
        b = self.val(1, LAG[stage])
        return b // NBLK

    def blk(self, stage):
        b = self.val(1, LAG[stage])
        return b % NBLK

    def prev(self):
        return It(self.base - 1, self.k)


def fills(step, it):
    bank, n = BANK[step], 0
    for s, b, stage in STEPS:
        if b != bank:
            continue
        upto = it.base if [x[0] for x in STEPS].index(s) <= [x[0] for x in STEPS].index(step) else it.base - 1
        n += max(0, min(upto + LAG[stage], LIMIT[stage] - 1) + 1)
    if it.k is None:
        return n
    assert it.base >= 2
    return it.k * (2 * sum(b == bank for _, b, _ in STEPS)) + n


def wait(eng, sem, value):
    if isinstance(value, int) and value <= 0:
        return
    eng.wait_ge(sem, value)


def norm_number(kind, p):
    if p < 6:
        return NORM_ATTN + 4 * (p // 2) + 2 * (kind - 1) + p % 2
    if p == 6:
        return NORM_ATTN + 12 + kind - 1
    return NORM_Q if kind == 1 else NORM_Q + 2


def norm_of_step(it, back=0):
    if it.k is None and it.base - back < 3:
        return (NORM_Q - 2, NORM_Q - 1, NORM_Q + 1)[it.base - back]
    return it.val(1, NORM_Q - back)


def parity_of_step(it, back=0):
    return norm_of_step(It(it.base), back) % 2


def pairs(eng, first, loop_from, loops, last, body):
    for j in range(first, loop_from):
        body(It(j))
    with eng.Fori(0, loops) as k:
        for par in range(2):
            body(It(loop_from + par, k))
    for j in range(loop_from + 2 * loops, last + 1):
        body(It(j))


def wait_apart(eng, sem, value, scratch):
    wait(eng, sem, value)
    eng.memset(scratch, 0.0)


def sandwich(nc, x, Wq, bq, Wk, bk, Wv, bv, Wo, bo, omega, g1, be1, W1, bf1, W2, bf2, g2, be2,
             qw, qscale, qbias, lora_a, lora_b, ln_g, ln_b, out):
    ctx = ExitStack()

    def sb(name, shape, dt=F32):
        return ctx.enter_context(nc.sbuf_tensor(name, shape, dt))

    def sem(name):
        return ctx.enter_context(nc.semaphore(name))

    with ctx:
        XT = sb("x_feat", [128, NBLK, TOK])
        XK = sb("x_tok", [128, NBLK, SEQ, D])
        WA = sb("w_rec_a", [128, LAYERS, RA])
        WC = sb("w_rec_c", [128, LAYERS, RC])
        WV = sb("w_v", [128, LAYERS, D])
        WO = sb("w_o", [128, LAYERS, D])
        WD = sb("w_2", [128, 2, FT, D])
        BV = sb("bv_rows", [128, LAYERS, D])
        BO = sb("bo_rows", [128, LAYERS + 1, D])
        G1 = sb("g1_rows", [128, 2, D])
        BE1 = sb("be1_rows", [128, 2, D])
        BF2 = sb("bf2_rows", [128, 2, D])
        G2 = sb("g2_rows", [128, 2, D])
        BE2 = sb("be2_rows", [128, 2, D])
        WE = sb("w_eff", [128, 2 * QBLK, D])
        QB = sb("q_bias_rows", [128, 2 * QBLK, D])
        QG = sb("q_gamma_beta", [128, 2, QBLK])
        IDN = sb("identity", [128, 128])
        TRI = sb("causal", [128, 128])
        BDM = sb("head_blocks", [128, 128])
        HM8 = sb("head_of_row", [128, HT_])
        PARM = sb("head_parity", [128, 2])
        KEEP = sb("keep_state", [128, TASKS + 1])
        NHALF = sb("minus_half", [128, SEQ])
        CA = sb("cur_a", [128, RA - 256])
        CAH = sb("cur_qk_hi", [128, 256], F32R)
        CAL = sb("cur_qk_lo", [128, 256], F32R)
        CCH = sb("cur_w1_hi", [128, FF], F32R)
        CCL = sb("cur_w1_lo", [128, FF], F32R)
        CB = sb("cur_bf1", [128, FT])
        XS = sb("x_feat_cur", [128, TOK])
        XH = sb("x_feat_hi", [128, TOK], F32R)
        XL = sb("x_feat_lo", [128, TOK], F32R)
        PQ = sb("phi_q", [128, 2, 2, TOK])
        PK = sb("phi_k", [128, 2, TOK])
        QEH = sb("phi_q_parity_hi", [128, SEQ, 2, 2, CH], F32R)
        QEL = sb("phi_q_parity_lo", [128, SEQ, 2, 2, CH], F32R)
        KH = sb("phi_k_hi", [128, 2, TOK], F32R)
        KL = sb("phi_k_lo", [128, 2, TOK], F32R)
        KTK = sb("phi_k_tok", [128, SEQ, 2, 128])
        VP = sb("v_padded", [128, 2, SEQ, HEADS, 32])
        SM = sb("scores_masked", [128, 2, 4, 4, CH])
        SF = sb("state_full", [128, SEQ, 2, 128])
        SK = sb("state_masked", [128, SEQ, 2, 128])
        MK = sb("keep_blocks", [128, 128])
        OS = sb("attn_num_den", [128, SEQ, 2, CH])
        DN = sb("den", [128, 2, 32])
        AK = sb("attn_tok", [128, SEQ, D])
        AF = sb("attn_feat", [128, TOK])
        R = sb("ln_in", [128, SEQ, D])
        N = sb("ln_out", [128, SEQ, D])
        ST = sb("ln_stats", [128, SEQ, 6])
        MV = sb("ln_mean_var", [128, SEQ, 2])
        VE = sb("ln_var_eps", [128, SEQ])
        RS = sb("ln_rstd", [128, SEQ])
        NM = sb("ln_minus_mean", [128, SEQ])
        SHF = sb("ln_shift", [128, SEQ])
        H1 = sb("h1_tok", [128, SEQ, D])
        H1B = sb("h1_bias_tok", [128, SEQ, D])
        HFH = sb("h1_feat_hi", [128, TOK], F32R)
        HFL = sb("h1_feat_lo", [128, TOK], F32R)
        Y = sb("ff_feat", [128, FT, TOK])
        QS = Y
        X2 = sb("x_tok_cur", [128, SEQ, D])
        CARRY = sb("wait_carrier", [128, 2])
        NMV = sb("norm_mean_var", [128, 2, SEQ, 2])
        NNM = sb("norm_minus_mean", [128, 2, SEQ])
        NVE = sb("norm_var_eps", [128, 2, SEQ])
        NRS = sb("norm_rstd", [128, 2, SEQ])
        NSH = sb("norm_shift", [128, 2, SEQ])
        P = ctx.enter_context(nc.psum_tensor("banks", [128, 8, 512], F32))

        def rows(table, l):
            return table[:, l, :].unsqueeze(1).to_broadcast([128, SEQ, D])

        x_dram = [x[s].rearrange("(p i) f -> i p f", i=CH) for s in range(SEQ)]
        out_dram = [out[s].rearrange("(p i) f -> i p f", i=CH) for s in range(SEQ)]

        x_first = sem("x_first"); x_rest = sem("x_rest")
        om_in = sem("omega_in"); wa_in = sem("w_a_in"); bo_in = sem("bo_in"); wv_in = sem("w_v_in")
        w_in = sem("w_in"); q_tables_in = sem("q_tables_in"); q_in = sem("q_in"); x0_in = sem("x0_in")
        consts = sem("consts"); zeroed = sem("zeroed")
        om_step = sem("om_step"); bias_done = sem("bias_done")
        n_stats = sem("norm_stats_ready")
        n_mv = sem("norm_mean_var_ready")
        n_var = sem("norm_var_ready")
        n_rstd = sem("norm_rstd_ready")
        n_shift = sem("norm_shift_ready")
        n_out = sem("norm_out_ready")
        pre_t = sem("input_transposed"); pre_xt = sem("input_feat_ready"); pre_xk = sem("input_tok_ready")
        dq_step = sem("dequantised"); lb_t = sem("lora_b_transposed"); lb_sb = sem("lora_b_ready")
        we_ps = sem("w_eff_full"); we_sb = sem("w_eff_ready")
        x1_ready = sem("x1_ready")
        h_ready = sem("h_ready")
        hs_ready = sem("h_cur_ready")
        hb_ready = sem("h_bias_ready")
        ht_full = sem("h_feat_full"); ht_copied = sem("h_feat_ready")
        l1_full = sem("first_product_full"); l1_added = sem("first_product_ready")
        gt_full = sem("normed_feat_full"); gelu_done = sem("gelu_ready"); l2_full = sem("second_product_full")
        out_ready = sem("out_ready"); stored = sem("stored")

        OMR = Y[0:64, 0, 0:LAYERS * M2].rearrange("p (l m) -> p l m", l=LAYERS)
        NW = 2 * QBLK
        spare = VP[:, :, :, :, :].rearrange("p a b c d -> p (a b c d)")[:, 4 * TOK:]
        QI = spare[:, 0:NW * D].rearrange("p (w d) -> p w d", w=NW).bitcast(I32)
        QW = spare[:, NW * D:2 * NW * D].rearrange("p (w d) -> p w d", w=NW)
        LA = PK[0:32, :, :].rearrange("p a b -> p (a b)")[:, 0:NW * D].rearrange("p (w d) -> p w d", w=NW)
        LBT = PQ[0:32, 0].rearrange("p a b -> p (a b)")[:, 0:NW * D].rearrange("p (w d) -> p w d", w=NW)
        QSC = XS[:, 0:8 * NW].rearrange("p (w g) -> p w g", w=NW)
        LB = XS[:, 64:64 + 32 * NW].rearrange("p (w r) -> p w r", w=NW)
        XN = (X2, H1)
        X1 = XT[:, :, :].rearrange("p n (s e) -> p n s e", s=SEQ)
        HB = VP[:, 0].rearrange("p a b c -> p (a b c)").rearrange("p (n s e) -> p n s e", n=4, s=SEQ)
        free = SM[:, :, :, :, :].rearrange("p a b c d -> p (a b c d)").rearrange("p (n t) -> p n t", n=8)
        HS = free[:, 0].rearrange("p (s e) -> p s e", s=SEQ)
        RQ = [free[:, 1 + j].rearrange("p (s e) -> p s e", s=SEQ) for j in range(2)]
        NQ = [free[:, 3 + j].rearrange("p (s e) -> p s e", s=SEQ) for j in range(2)]
        HFQ = free[:, 5]
        GF = free[:, 6]

        filled = {b: sem(f"bank{b}_filled") for b in (5, 6, 7)}
        drained = {b: sem(f"bank{b}_drained") for b in (5, 6, 7)}
        scores_full = sem("scores_full")
        scores_masked = sem("scores_masked")
        av_done = sem("av_done")
        o_copied = sem("o_copied")
        state_full = sem("state_full")
        state_added = sem("state_added")
        state_ready = sem("state_ready")
        keep_ready = sem("keep_ready")
        qk_hi = sem("scores_operands_hi")
        qk_lo = sem("scores_operands_lo")
        hf_hi = sem("h1_feat_hi_ready")
        wcl_ready = sem("w1_lo_ready")
        xs_ready = sem("xs_ready")
        wa_ready = sem("wa_ready")
        wal_ready = sem("w_qk_lo_ready")
        xh_ready = sem("x_hi_ready")
        xl_ready = sem("x_lo_ready")
        wc_ready = sem("wc_ready")
        den_step = sem("den_step")
        ln_in = sem("ln_in_ready")
        ln_stats = sem("ln_stats_ready")
        ln_mv = sem("ln_mean_var_ready")
        ln_var = sem("ln_var_eps_ready")
        ln_rstd = sem("ln_rstd_ready")
        ln_nm = sem("ln_minus_mean_ready")
        ln_shift = sem("ln_shift_ready")
        ln_norm = sem("ln_norm_ready")
        ln_gain = sem("ln_gain_ready")
        ln_out = sem("ln_out_ready")
        h1b_ready = sem("h1b_ready")
        xk_ready = sem("xk_ready")

        def full(eng, step, it):
            wait(eng, filled[BANK[step]], fills(step, it))

        def layer_loaded(eng, it):
            wait(eng, w_in, it.layer("C") * W_LAYER + (W_DMAS - W_LAYER))

        def emptied(eng, step, it):
            wait(eng, drained[BANK[step]], fills(step, it))

        def claim(eng, step, it):
            n = fills(step, it)
            wait(eng, drained[BANK[step]], n - 1 if isinstance(n, int) else n + -1)

        def pipeline(eng, body):
            pairs(eng, FIRST, LOOP0, LOOPS, LAST, body)

        def v_dense(par, s, t):
            v = VP[:, par, s, HT_ * t:HT_ * t + HT_, :].rearrange("p (a b) (q c) -> p a (b q) c", b=2, c=SLOT)
            return v[:, :, 0::3, :]

        def bank4(s):
            return P[:, 4, 256 * (s % 2):256 * (s % 2) + 256].rearrange("p (t i) -> p t i", t=2)

        with nc.Block() as block:
            @block.sync
            def _(sp):
                blocks = x.rearrange("s (p i) f -> p i s f", i=CH)
                sp.dma_start(XK[:, 0], blocks[0]).then_inc(x_first, 16)
                for s in range(SEQ):
                    sp.dma_start(XK[:, 1:, s, :], x_dram[s][:, 1:, :]).then_inc(x_rest, 16)
                sp.dma_start(BO[:, 0:LAYERS, :], bo.partition_broadcast(128)).then_inc(bo_in, 16)
                sp.dma_start(WV[:, :, :], Wv.rearrange("l d e -> d l e")).then_inc(wv_in, 16)
                sp.dma_start(BV[:, :, :], bv.partition_broadcast(128)).then_inc(wv_in, 16)
                sp.dma_start(WO[:, :, :], Wo.rearrange("l d e -> d l e")).then_inc(w_in, 16)
                sp.dma_start(WC[:, :, 0:FF], W1.rearrange("l d f -> d l f")).then_inc(w_in, 16)
                with nc.allow_non_contiguous_dma(reason="small tables by feature"):
                    for t in range(FT):
                        sp.dma_start(WC[:, :, FF + t], bf1[:, 128 * t:128 * t + 128].rearrange("l f -> f l")) \
                            .then_inc(w_in, 16)
                for t in range(FT):
                    sp.dma_start(WD[:, :, t, :], W2[0:2, 128 * t:128 * t + 128, :].rearrange("l f d -> f l d")) \
                        .then_inc(w_in, 16)
                for table, src in ((G1, g1), (BE1, be1), (BF2, bf2), (G2, g2), (BE2, be2)):
                    sp.dma_start(table[:, :, :], src[0:2].partition_broadcast(128)).then_inc(w_in, 16)
                sp.dma_start(QB[:, :, :], qbias.partition_broadcast(128)).then_inc(q_tables_in, 16)
                with nc.allow_non_contiguous_dma(reason="small tables by feature"):
                    sp.dma_start(QG[:, 0, :], ln_g.rearrange("l f -> f l")).then_inc(q_tables_in, 16)
                    sp.dma_start(QG[:, 1, :], ln_b.rearrange("l f -> f l")).then_inc(q_tables_in, 16)
                for l in range(2, LAYERS):
                    wait(sp, xk_ready, NBLK * (l - 1) + 1)
                    for t in range(FT):
                        sp.dma_start(WD[:, l % 2, t, :], W2[l, 128 * t:128 * t + 128, :]).then_inc(w_in, 16)
                    for table, src in ((G1, g1), (BE1, be1), (BF2, bf2), (G2, g2), (BE2, be2)):
                        sp.dma_start(table[:, l % 2, :], src[l].partition_broadcast(128)).then_inc(w_in, 16)
                emptied(sp, "XD", It(LOOP0 + 2 * LOOPS - 1))
                for p in range(NBLK):
                    last_read = It(TASKS - NBLK + p - 1)
                    full(sp, "QP", last_read)
                    full(sp, "KP", last_read)
                    wait(sp, xs_ready, TASKS - NBLK + p + 1)
                    wait(sp, x0_in, 16 * p)
                    sp.dma_start(X1[:, p], blocks[p]).then_inc(x0_in, 16)
                wait(sp, av_done, SEQ * TASKS)
                wait(sp, qk_lo, 3 * SEQ * TASKS)
                full(sp, "KT1", It(TASKS - 2))
                full(sp, "VP", It(TASKS - 2))
                sp.dma_start(QI, qw.rearrange("w o d -> o w d")).then_inc(q_in, 16)
                sp.dma_start(QSC, qscale.rearrange("w o g -> o w g")).then_inc(q_in, 16)
                sp.dma_start(LA, lora_a.rearrange("w r d -> r w d")).then_inc(q_in, 16)
                sp.dma_start(LB, lora_b.rearrange("w o r -> o w r")).then_inc(q_in, 16)
                out_blocks = out.rearrange("s (p i) f -> p i s f", i=CH)
                for p in range(NBLK):
                    sp.wait_ge(out_ready, p + 1)
                    sp.dma_start(out_blocks[p], XK[:, p]).then_inc(stored, 16)
                sp.wait_ge(stored, 16 * NBLK)

            @block.tensor
            def _(pe):
                pe.wait_ge(consts, 4)

                def transpose_input(it):
                    wait(pe, n_out, it.val(1, NORM_IN + 1))
                    wait(pe, pre_xt, it.val(1, -1))
                    for s in range(SEQ):
                        ins = nc.tensor.transpose(P[:, it.base % 2, CH * s:CH * s + CH], XN[it.base % 2][:, s, :],
                                                  IDN[:, :])
                    ins.then_inc(pre_t, 1)

                pairs(pe, 0, 2, NBLK // 2 - 1, NBLK - 1, transpose_input)
                pe.wait_ge(pre_xt, NBLK)

                def fill(step, it, ins):
                    ins.then_inc(filled[BANK[step]], 1)

                def scores(it, s, half):
                    if half == 0:
                        wait(pe, qk_lo, it.val(3 * SEQ, 3 * s + 3))
                    for n, (key, query) in enumerate(((KH, QEH), (KH, QEL), (KL, QEH))):
                        for g in range(4):
                            if half == 0 and n == 0:
                                wait(pe, scores_masked, it.val(16, 4 * (s - 1) + g + 1))
                            rg = slice(32 * g, 32 * g + 32)
                            ins = nc.tensor.matmul(P[:, g, 2 * CH * half:2 * CH * half + 2 * CH],
                                                   key[rg, half, CH * s:CH * s + CH],
                                                   query[rg, s, half].rearrange("p a i -> p (a i)"),
                                                   start=(n == 0), stop=(n == 2), skip_group_check=True)
                    if half == 1:
                        ins.then_inc(scores_full, 1)

                def attend(it, s):
                    par = it.par("B")
                    o = bank4(s)
                    if s == 0:
                        emptied(pe, "VP", it.prev())
                        wait(pe, state_ready, it.val(2, 0))
                        wait(pe, state_added, it.val(2, 0))
                    if s == 2 and it.base < TASKS - 1:
                        wait(pe, state_added, it.val(2, 1))
                    if s == 2 and it.base == TASKS - 1:
                        wait(pe, o_copied, it.val(2, 1))
                    for t in range(2):
                        nc.tensor.matmul(o[:, t, :], SK[:, s, t, :], PQ[:, par, t, CH * s:CH * s + CH],
                                         start=(t == 0), stop=False, skip_group_check=True)
                    wait(pe, scores_masked, it.val(16, 4 * s + 4))
                    for sub in range(4):
                        for g in range(4):
                            t, h = sub // 2, 8 * (sub // 2) + 2 * g + sub % 2
                            ins = nc.tensor.matmul(o[32 * g:32 * g + 32, t, :], VP[:, par, s, h, :],
                                                   SM[:, s % 2, g, sub, :], start=False, stop=(sub % 2 == 1),
                                                   skip_group_check=True)
                    ins.then_inc(av_done, 1)

                def state(it, j):
                    par = it.par("B")
                    if j == 0:
                        emptied(pe, "KT1", it.prev())
                    wait(pe, o_copied, it.val(2, 1 + j))
                    for s in (2 * j, 2 * j + 1):
                        for t in range(2):
                            ins = nc.tensor.matmul(bank4(s)[:, t, :], KTK[:, s, t, :], v_dense(par, s, t),
                                                   start=True, stop=True, skip_group_check=True)
                    ins.then_inc(state_full, 1)

                def project(it, step, col):
                    claim(pe, step, it)
                    if step == "QP":
                        wait(pe, wa_ready, it.val(2, 4))
                        wait(pe, wal_ready, it.val(1, 2))
                        wait(pe, xl_ready, it.val(1, 2))
                    for n, (w, xp) in enumerate(((CAH, XH), (CAH, XL), (CAL, XH))):
                        ins = nc.tensor.matmul(P[:, BANK[step], :], w[:, col:col + 128], xp[:, :],
                                               start=(n == 0), stop=(n == 2))
                    fill(step, it, ins)

                def logits(it, step, n):
                    claim(pe, step, it)
                    emptied(pe, "QP" if n < 2 else "KP", it)
                    fill(step, it, nc.tensor.matmul(P[:, BANK[step], :], CA[:, 0:128], QS[:, n, :],
                                                    start=True, stop=True))

                def transposes(it, step, srcs):
                    claim(pe, step, it)
                    for n, src in enumerate(srcs):
                        ins = nc.tensor.transpose(P[:, BANK[step], CH * n:CH * n + CH], src, IDN[:, :])
                    fill(step, it, ins)

                def first_product(it, f):
                    step = f"W1_{f}"
                    claim(pe, step, it)
                    for n, (w, h) in enumerate(((CCH, HFH), (CCH, HFL), (CCL, HFH))):
                        ins = nc.tensor.matmul(P[:, BANK[step], :], w[:, 128 * f:128 * f + 128], h[:, :],
                                               start=(n == 0), stop=(n == 2))
                    fill(step, it, ins)

                def lora_b_by_rank():
                    pe.wait_ge(q_in, 64)
                    pe.wait_ge(scores_masked, 16 * TASKS)
                    for w in range(NW):
                        ins = nc.tensor.transpose(P[0:32, w // 4, D * (w % 4):D * (w % 4) + D], LB[:, w, :], IDN[:, :])
                    ins.then_inc(lb_t, 1)

                def effective_weights():
                    pe.wait_ge(dq_step, 2)
                    pe.wait_ge(lb_sb, 2)
                    for w in range(NW):
                        dst = P[:, 2 + w // 4, D * (w % 4):D * (w % 4) + D]
                        nc.tensor.matmul(dst, QW[:, w, :], IDN[:, :], start=True, stop=False)
                        ins = nc.tensor.matmul(dst, LA[:, w, :], LBT[:, w, :], start=False, stop=True)
                    ins.then_inc(we_ps, 1)

                def q_step(it):
                    if it.base >= 3:
                        pe.wait_ge(n_out, norm_of_step(it, 3) + 1)
                        wait(pe, gelu_done, it.val(1, -3))
                        for s in range(SEQ):
                            ins = nc.tensor.transpose(P[:, 1, CH * s:CH * s + CH], NQ[(it.base - 3) % 2][:, s, :],
                                                      IDN[:, :])
                        ins.then_inc(gt_full, 1)
                    if 0 <= it.base < STEPS_Q:
                        pe.wait_ge(ht_copied, it.val(1, 1))
                        wait(pe, l1_added, it.val(1, 0))
                        for s in range(SEQ):
                            ins = nc.tensor.matmul(P[:, 2, CH * s:CH * s + CH], HFQ[:, CH * s:CH * s + CH],
                                                   WE[:, it.val(1, 0) // NBLK * 2, :], start=True, stop=True)
                        ins.then_inc(l1_full, 1)
                    if it.base + 1 < STEPS_Q:
                        pe.wait_ge(hs_ready, it.val(1, 2))
                        wait(pe, ht_copied, it.val(1, 1))
                        for s in range(SEQ):
                            ins = nc.tensor.transpose(P[:, 0, CH * s:CH * s + CH], HS[:, s, :], IDN[:, :])
                        ins.then_inc(ht_full, 1)
                    if it.base >= 3:
                        pe.wait_ge(gelu_done, it.val(1, -2))
                        if it.base >= 4:
                            pe.wait_ge(h_ready, it.val(1, NBLK - 3))
                        for s in range(SEQ):
                            ins = nc.tensor.matmul(P[:, 3, CH * s:CH * s + CH], GF[:, CH * s:CH * s + CH],
                                                   WE[:, it.val(1, -3) // NBLK * 2 + 1, :], start=True, stop=True)
                        ins.then_inc(l2_full, 1)

                def layers(it):
                    A, B, C, Dd = (it.active(x) for x in "ABCD")
                    if it.base == 0:
                        pe.wait_ge(consts, ALL_CONSTS)
                    if it.base == 1:
                        pe.wait_ge(w_in, W_DMAS)
                    if B:
                        scores(it, 0, 0)
                    if C:
                        for j in range(2):
                            wait(pe, o_copied, it.val(2, j - 1))
                            transposes(it, f"T{j}", [OS[:, s, t, :] for s in (2 * j, 2 * j + 1) for t in range(2)])
                    if it.base == TASKS:
                        lora_b_by_rank()
                    if A:
                        project(it, "QP", 0)
                    if B:
                        scores(it, 0, 1)
                    if A:
                        project(it, "KP", 128)
                    if C:
                        emptied(pe, "T0", it)
                        emptied(pe, "T1", it)
                        transposes(it, "AT", [AK[:, s, :] for s in range(SEQ)])
                    if A:
                        logits(it, "LQ0", 0)
                        logits(it, "LQ1", 1)
                    if B:
                        scores(it, 1, 0)
                    if C:
                        claim(pe, "WO", it)
                        emptied(pe, "AT", it)
                        for s in range(SEQ):
                            ins = nc.tensor.matmul(P[:, BANK["WO"], CH * s:CH * s + CH], AF[:, CH * s:CH * s + CH],
                                                   WO[:, it.layer("C"), :], start=True, stop=True)
                        fill("WO", it, ins)
                    if it.base == TASKS:
                        effective_weights()
                        q_step(It(-1))
                    if B:
                        scores(it, 1, 1)
                    if A:
                        logits(it, "LK0", 2)
                    if B:
                        attend(it, 0)
                    if A:
                        logits(it, "LK1", 3)
                    if B:
                        scores(it, 2, 0)
                    if A:
                        claim(pe, "VP", it)
                        if it.base == FIRST:
                            pe.wait_ge(wv_in, 32)
                        wait(pe, xs_ready, it.val(1, 2))
                        for s in range(SEQ):
                            ins = nc.tensor.matmul(P[:, BANK["VP"], CH * s:CH * s + CH], XS[:, CH * s:CH * s + CH],
                                                   WV[:, it.layer("A"), :], start=True, stop=True)
                        fill("VP", it, ins)
                    if B:
                        scores(it, 2, 1)
                    if C:
                        wait(pe, ln_out, it.val(2, -1))
                        transposes(it, "HT", [H1[:, s, :] for s in range(SEQ)])
                    if it.base == TASKS:
                        pe.wait_ge(we_sb, 2)
                        q_step(It(0))
                    if B:
                        attend(it, 1)
                    if Dd:
                        transposes(it, "XD", [X2[:, s, :] for s in range(SEQ)])
                    if C:
                        wait(pe, wcl_ready, it.val(1, 0))
                        emptied(pe, "HT", it)
                        first_product(it, 0)
                    if B and it.base < TASKS - 1:
                        state(it, 0)
                    if B:
                        scores(it, 3, 0)
                    if C:
                        first_product(it, 1)
                    if B:
                        scores(it, 3, 1)
                    if C:
                        first_product(it, 2)
                    if B:
                        attend(it, 2)
                    if C:
                        first_product(it, 3)
                    if B:
                        attend(it, 3)
                    if C:
                        claim(pe, "W2", it)
                        layer_loaded(pe, it)
                        emptied(pe, "W1_2", it)
                        emptied(pe, "W1_3", it)
                        for s in range(SEQ):
                            for f in range(FT):
                                ins = nc.tensor.matmul(P[:, BANK["W2"], CH * s:CH * s + CH],
                                                       Y[:, f, CH * s:CH * s + CH], WD[:, it.layer("C") % 2, f, :],
                                                       start=(f == 0), stop=(f == FT - 1))
                        fill("W2", it, ins)
                    if B and it.base < TASKS - 1:
                        state(it, 1)
                    if A:
                        emptied(pe, "LK0", it)
                        emptied(pe, "LK1", it)
                        for j in range(2):
                            transposes(it, f"KT{j}", [PK[:, t, CH * s:CH * s + CH]
                                                      for s in (2 * j, 2 * j + 1) for t in range(2)])

                pipeline(pe, layers)
                pairs(pe, 1, *STEADY_Q, STEPS_Q + 2, q_step)

            @block.scalar
            def _(act):
                for h in range(HT_):
                    act.dma_start(OMR[8 * h:8 * h + 8], omega.rearrange("l d m -> d l m")).then_inc(om_in, 16)
                act.dma_start(WA[:, :, 0:128], Wq.rearrange("l d e -> d l e")).then_inc(wa_in, 16)
                act.dma_start(WA[:, :, 128:256], Wk.rearrange("l d e -> d l e")).then_inc(wa_in, 16)
                with nc.allow_non_contiguous_dma(reason="small tables by feature"):
                    act.dma_start(WA[:, :, 384], bq.rearrange("l e -> e l")).then_inc(wa_in, 16)
                    act.dma_start(WA[:, :, 385], bk.rearrange("l e -> e l")).then_inc(wa_in, 16)

                def norm(n, par, dst, src):
                    wait(act, n_shift, n + 1)
                    for s in range(SEQ):
                        ins = nc.scalar.activation(dst[:, s, :], src[:, s, :], ACT.Identity,
                                                   bias=NSH[:, par, s:s + 1], scale=NRS[:, par, s:s + 1])
                    ins.then_inc(n_out, 1)

                def norm_input(it):
                    wait(act, pre_t, it.val(1, -1))
                    wait(act, pre_xk, it.val(1, -1))
                    norm(it.val(1, NORM_IN), it.base % 2, XN[it.base % 2], XK[:, it.val(1, 0)])

                pairs(act, 0, 2, NBLK // 2 - 1, NBLK - 1, norm_input)

                def copy_out(it, step, dst, func=ACT.Copy, **kw):
                    full(act, step, it)
                    nc.scalar.activation(dst, P[:, BANK[step], :], func, **kw).then_inc(drained[BANK[step]], 1)

                def front(kind, p):
                    n = norm_number(kind, p)
                    norm(n, n % 2, XK[:, p], XK[:, p] if kind == 1 else X1[:, p])

                def lora_b_by_rank():
                    act.wait_ge(lb_t, 1)
                    for i, ws in enumerate((slice(0, 4), slice(4, NW))):
                        nc.scalar.activation(LBT[:, ws, :].rearrange("p w d -> p (w d)"),
                                             P[0:32, i, 0:D * (ws.stop - ws.start)], ACT.Copy).then_inc(lb_sb, 1)

                def effective_weights():
                    act.wait_ge(we_ps, 1)
                    for i, ws in enumerate((slice(0, 4), slice(4, NW))):
                        nc.scalar.activation(WE[:, ws, :].rearrange("p w d -> p (w d)"),
                                             P[:, 2 + i, 0:D * (ws.stop - ws.start)], ACT.Copy).then_inc(we_sb, 1)

                def lines_squares(it, step, n):
                    full(act, step, it)
                    src, col = P[:, BANK[step], :], 128 + n
                    for half in range(2):
                        hr = slice(64 * half, 64 * half + 64)
                        nc.scalar.activation(QS[0:64, 2 * n + half, :], src[hr, :], ACT.Identity,
                                             bias=CA[hr, col:col + 1], scale=S_X)
                        ins = nc.scalar.activation(QS[64:128, 2 * n + half, :], src[hr, :], ACT.Square,
                                                   bias=CA[hr, col:col + 1], scale=S_X)
                    ins.then_inc(drained[BANK[step]], 1)

                def normalise_1(it):
                    wait(act, ln_shift, it.val(1, 0))
                    wait(act, ln_out, it.val(2, -2))
                    for s in range(SEQ):
                        ins = nc.scalar.activation(N[:, s, :], R[:, s, :], ACT.Identity, bias=SHF[:, s:s + 1],
                                                   scale=RS[:, s:s + 1])
                    ins.then_inc(ln_norm, 1)

                def operands_hi(it, s):
                    wait(act, scores_full, it.val(4, s + 1))
                    i = slice(CH * s, CH * s + CH)
                    for par in range(2):
                        nc.scalar.activation(QEH[:, s, :, par, :], PQ[:, it.par("A"), :, i], ACT.Identity,
                                             scale=PARM[:, par:par + 1]).then_inc(qk_hi, 1)
                    nc.scalar.activation(KH[:, :, i], PK[:, :, i], ACT.Copy).then_inc(qk_hi, 1)

                def attn_copy(it, j):
                    wait(act, av_done, it.val(4, 2 * j + 2))
                    nc.scalar.activation(OS[:, 2 * j:2 * j + 2].rearrange("p a b c -> p (a b c)"), P[:, 4, :],
                                         ACT.Copy).then_inc(o_copied, 1)

                def norm_step(it, back):
                    j = (it.base - back) % 2
                    wait(act, gt_full, it.val(1, -back - 1))
                    norm(norm_of_step(it, back), parity_of_step(it, back), NQ[j], RQ[j])

                def q_step(it):
                    if it.base >= 3:
                        blk = it.val(1, -3) // NBLK
                        act.wait_ge(gt_full, it.val(1, -2))
                        wait(act, l2_full, it.val(1, -3))
                        nc.scalar.activation(GF[:, :], P[:, 1, :], ACT.Gelu, bias=QG[:, 1, bass.ds(blk, 1)],
                                             scale=QG[:, 0, bass.ds(blk, 1)]).then_inc(gelu_done, 1)
                    if it.base + 1 < STEPS_Q:
                        act.wait_ge(ht_full, it.val(1, 2))
                        wait(act, l1_full, it.val(1, 1))
                        nc.scalar.activation(HFQ[:, :], P[:, 0, :], ACT.Copy).then_inc(ht_copied, 1)
                    if 3 <= it.base <= STEPS_Q:
                        norm_step(it, 1)

                def weights_a(l):
                    nc.scalar.activation(CAH[:, :], WA[:, l, 0:256], ACT.Copy).then_inc(wa_ready, 1)
                    nc.scalar.activation(CA[:, :], WA[:, l, 256:RA], ACT.Copy).then_inc(wa_ready, 1)

                def input_hi(blk):
                    nc.scalar.activation(XH[:, :], XT[:, blk, :], ACT.Copy).then_inc(xh_ready, 1)

                def layers(it):
                    A, B, C, Dd = (it.active(x) for x in "ABCD")
                    if A:
                        lines_squares(it, "QP", 0)
                    if C:
                        copy_out(it, "AT", AF[:, :])
                    if A:
                        lines_squares(it, "KP", 1)
                    if it.base == TASKS:
                        lora_b_by_rank()
                    if A:
                        copy_out(it, "LQ0", PQ[:, it.par("A"), 0, :], ACT.Exp)
                        copy_out(it, "LQ1", PQ[:, it.par("A"), 1, :], ACT.Exp)
                    if it.base < TASKS:
                        for p in FRONT.get(it.base, ()):
                            front(1, p)
                    if C:
                        normalise_1(it)
                    if A:
                        wait(act, qk_lo, it.val(3 * SEQ, 3 * SEQ))
                        copy_out(it, "LK0", PK[:, 0, :], ACT.Exp)
                        copy_out(it, "LK1", PK[:, 1, :], ACT.Exp)
                        if it.base + 2 < TASKS:
                            emptied(act, "KP", it)
                            weights_a(it.val(1, 2) // NBLK)
                        if it.base == FIRST:
                            act.wait_ge(consts, ALL_CONSTS)
                        emptied(act, "LK0", it)
                        emptied(act, "LK1", it)
                        operands_hi(it, 0)
                        operands_hi(it, 1)
                    if it.base == TASKS:
                        effective_weights()
                        act.wait_ge(av_done, SEQ * TASKS)
                        q_step(It(-1))
                        for p in FRONT[TASKS]:
                            front(1, p)
                    if C:
                        full(act, "HT", it)
                        nc.scalar.activation(HFH[:, :], P[:, BANK["HT"], :], ACT.Copy).then_inc(hf_hi, 1)
                    if B:
                        attn_copy(it, 0)
                    if Dd:
                        copy_out(it, "XD", XT[:, it.blk("D"), :])
                    if C:
                        copy_out(it, "W1_0", Y[:, 0, :], ACT.Relu, bias=CB[:, 0:1])
                    if A:
                        operands_hi(it, 2)
                    if C:
                        for f in range(1, FT):
                            copy_out(it, f"W1_{f}", Y[:, f, :], ACT.Relu, bias=CB[:, f:f + 1])
                    if A and it.base + 2 < TASKS:
                        emptied(act, "XD", it.prev())
                        input_hi(it.val(1, 2) % NBLK)
                    if it.base == TASKS:
                        q_step(It(0))
                    for p in FRONT.get(it.base, ())[:1]:
                        front(2, p)
                    if B:
                        if it.base == 0:
                            act.wait_ge(w_in, W_DMAS)
                        emptied(act, "W1_2", it)
                        emptied(act, "W1_3", it)
                        l = it.val(1, 0) // NBLK
                        nc.scalar.activation(CCH[:, :], WC[:, l, 0:FF], ACT.Copy).then_inc(wc_ready, 1)
                        nc.scalar.activation(CB[:, :], WC[:, l, FF:RC], ACT.Copy).then_inc(wc_ready, 1)
                        attn_copy(it, 1)
                    if A:
                        operands_hi(it, 3)
                    for p in FRONT.get(it.base, ())[1:]:
                        front(2, p)
                    if A:
                        for j in range(2):
                            copy_out(it, f"KT{j}", KTK[:, 2 * j:2 * j + 2].rearrange("p a b c -> p (a b c)"))

                act.wait_ge(om_step, 3)
                act.wait_ge(bias_done, 1)
                weights_a(0)
                act.wait_ge(pre_xt, NBLK)
                input_hi(0)
                pipeline(act, layers)

                def norm_h(it):
                    h = XK[:, it.val(1, 0)]
                    norm(it.val(1, NORM_H), it.base % 2, h, h)

                act.wait_ge(q_tables_in, 48)
                nc.scalar.activation(CARRY[:, 1:2], QG[:, 0, 0:1], ACT.Gelu)
                q_step(It(1))
                norm_step(It(0), 0)
                q_step(It(2))
                norm_step(It(1), 0)
                front(1, 7)
                q_step(It(3))
                front(2, 7)
                pairs(act, 4, *STEADY_Q, STEPS_Q + 1, q_step)
                norm_h(It(0))
                q_step(It(STEPS_Q + 2))
                norm_h(It(1))
                pairs(act, 2, 2, NBLK // 2 - 1, NBLK - 1, norm_h)

            @block.vector
            def _(dve):
                nc.vector.memset(VP[:, :, :, :, :], 0.0).then_inc(zeroed, 1)
                nc.vector.memset(SK[:, :, :, :], 0.0).then_inc(zeroed, 1)
                nc.vector.memset(SF[:, :, :, :], 0.0).then_inc(zeroed, 1)

                def norm_statistics(n, par, src):
                    for s in range(SEQ):
                        nc.vector.bn_stats(ST[:, s, :], src[:, s, :]).then_inc(n_stats, 1)
                    wait(dve, n_var, 2 * n - 2 if isinstance(n, int) else 2 * n + -2)
                    wait_apart(dve, n_stats, 4 * n + 4, CARRY[:, 0:1])
                    for s in range(SEQ):
                        nc.vector.bn_aggr(NMV[:, par, s, :], ST[:, s, :]).then_inc(n_mv, 1)
                    wait(dve, n_mv, 4 * n + 4)
                    wait(dve, n_shift, n - 1 if isinstance(n, int) else n + -1)
                    nc.vector.tensor_scalar(NNM[:, par, :], NMV[:, par, :, 0], -1.0, None, ALU.mult).then_inc(n_var, 1)
                    nc.vector.tensor_scalar(NVE[:, par, :], NMV[:, par, :, 1], LN_EPS, None, ALU.add).then_inc(n_var, 1)

                def input_block(it):
                    if it.base < NBLK:
                        norm_statistics(it.val(1, NORM_IN), it.base % 2, XK[:, it.val(1, 0)])
                    if it.base >= 2:
                        wait(dve, pre_t, it.val(1, -1))
                        nc.vector.tensor_copy(XT[:, it.val(1, -2), :], P[:, it.base % 2, :]).then_inc(pre_xt, 1)

                dve.wait_ge(x_first, 16)
                input_block(It(0))
                dve.wait_ge(x_rest, 16 * SEQ)
                input_block(It(1))
                dve.wait_ge(om_in, 16 * HT_)
                dve.wait_ge(consts, 8)
                om = WA[:, :, 256:384].rearrange("p l (h g m) -> p l h g m", h=HT_, g=2)
                nc.vector.tensor_tensor(om[0:64, :, :, 0, :],
                                        OMR[:, :, :].unsqueeze(2).to_broadcast([64, LAYERS, HT_, M2]),
                                        HM8[0:64, :].unsqueeze(1).unsqueeze(3).to_broadcast([64, LAYERS, HT_, M2]),
                                        ALU.mult).then_inc(om_step, 1)
                dve.wait_ge(om_step, 1)
                nc.vector.tensor_scalar(om[0:64, :, :, 1, :], om[0:64, :, :, 0, :], -1.0, None, ALU.mult) \
                    .then_inc(om_step, 1)
                nc.vector.tensor_scalar(WA[64:128, :, 256:384].rearrange("p l (h c) -> p l h c", h=HT_),
                                        HM8[64:128, :].unsqueeze(1).unsqueeze(3)
                                        .to_broadcast([64, LAYERS, HT_, 2 * M2]),
                                        -0.5, None, ALU.mult).then_inc(om_step, 1)

                pairs(dve, 2, 2, NBLK // 2 - 1, NBLK + 1, input_block)
                dve.wait_ge(wa_in, 64)
                nc.vector.tensor_scalar(WA[:, :, 384:386], WA[:, :, 384:386], S_X, None, ALU.mult) \
                    .then_inc(bias_done, 1)
                dve.wait_ge(pre_xt, NBLK)
                dve.wait_ge(pre_xk, NBLK)
                dve.wait_ge(consts, ALL_CONSTS)

                def mask(it, s, banks=range(4)):
                    wait(dve, scores_full, it.val(4, s + 1))
                    wait(dve, av_done, it.val(4, s - 1))
                    for g in banks:
                        nc.vector.tensor_tensor(SM[:, s % 2, g, :, :], P[:, g, :].rearrange("p (a i) -> p a i", a=4),
                                                TRI[:, :].unsqueeze(1).to_broadcast([128, 4, 128]),
                                                ALU.mult).then_inc(scores_masked, 1)

                def divide(it, j):
                    full(dve, f"T{j}", it)
                    t = P[:, BANK[f"T{j}"], :].rearrange("p (h c) -> p h c", c=SLOT)
                    nc.vector.tensor_scalar(DN[:, 0, :], t[:, :, DEN], DEN_EPS, None, ALU.add).then_inc(den_step, 1)
                    wait(dve, den_step, it.val(4, 2 * j - 3))
                    nc.vector.reciprocal(DN[:, 1, :], DN[:, 0, :]).then_inc(den_step, 1)
                    wait(dve, den_step, it.val(4, 2 * j - 2))
                    nc.vector.tensor_tensor(AK[:, 2 * j:2 * j + 2, :].rearrange("p s (h d) -> p (s h) d", d=DH),
                                            t[:, :, 0:DH], DN[:, 1, :].unsqueeze(2).to_broadcast([128, 32, DH]),
                                            ALU.mult).then_inc(drained[BANK[f"T{j}"]], 1)

                def statistics(it, n):
                    for s in range(SEQ):
                        nc.vector.bn_stats(ST[:, s, :], R[:, s, :]).then_inc(ln_stats, 1)
                    wait_apart(dve, ln_stats, it.val(8, 4 * n - 8), CARRY[:, 0:1])
                    for s in range(SEQ):
                        nc.vector.bn_aggr(MV[:, s, :], ST[:, s, :]).then_inc(ln_mv, 1)
                    wait(dve, ln_mv, it.val(8, 4 * n - 8))
                    nc.vector.tensor_scalar(VE[:, :], MV[:, :, 1], LN_EPS, None, ALU.add).then_inc(ln_var, 1)
                    if n == 1:
                        wait(dve, ln_shift, it.val(1, -1))
                        nc.vector.tensor_scalar(NM[:, :], MV[:, :, 0], -1.0, None, ALU.mult).then_inc(ln_nm, 1)

                def normalise_2(it):
                    wait(dve, ln_rstd, it.val(2, 0))
                    wait(dve, ln_out, it.val(2, -1))
                    for s in range(SEQ):
                        ins = nc.vector.tensor_scalar(N[:, s, :], R[:, s, :], MV[:, s, 0:1], RS[:, s:s + 1],
                                                      ALU.subtract, ALU.mult)
                    ins.then_inc(ln_norm, 1)

                def operands_lo(it, s):
                    wait(dve, qk_hi, it.val(3 * SEQ, 3 * SEQ + 3 * s + 3))
                    i = slice(CH * s, CH * s + CH)
                    for par in range(2):
                        nc.vector.scalar_tensor_tensor(QEL[:, s, :, par, :], PQ[:, it.par("A"), :, i],
                                                       PARM[:, par:par + 1], QEH[:, s, :, par, :].bitcast(F32),
                                                       ALU.mult, ALU.subtract).then_inc(qk_lo, 1)
                    nc.vector.tensor_tensor(KL[:, :, i], PK[:, :, i], KH[:, :, i].bitcast(F32), ALU.subtract) \
                        .then_inc(qk_lo, 1)

                def add_state(it, j):
                    wait(dve, state_full, it.val(2, 1 + j))
                    wait(dve, state_ready, it.val(2, j - 1))
                    m = it.val(1, 0)
                    sf = SF[:, 2 * j:2 * j + 2].rearrange("p a b c -> p (a b c)")
                    nc.vector.scalar_tensor_tensor(sf, sf, KEEP[:, bass.ds(m, 1)], P[:, 4, :],
                                                   ALU.mult, ALU.add).then_inc(state_added, 1)

                def values(it):
                    full(dve, "VP", it)
                    for s in range(SEQ):
                        dst = VP[:, it.par("A"), s].rearrange("p (a b) (q c) -> p a (b q) c", b=2, c=SLOT)
                        ins = nc.vector.tensor_tensor(
                            dst[:, :, 0::3, 0:DH],
                            P[:, BANK["VP"], CH * s:CH * s + CH].rearrange("p (a b d) -> p a b d", b=2, d=DH),
                            BV[:, it.layer("A"), :].rearrange("p (a b d) -> p a b d", b=2, d=DH), ALU.add)
                    ins.then_inc(drained[BANK["VP"]], 1)

                def residual(it, step, other):
                    full(dve, step, it)
                    nc.vector.tensor_tensor(R[:, :, :], P[:, BANK[step], :].rearrange("p (s e) -> p s e", s=SEQ),
                                            other, ALU.add).then_inc(drained[BANK[step]], 1)
                    emptied(dve, step, it)

                def front(kind, p):
                    n = norm_number(kind, p)
                    if kind == 1:
                        dve.wait_ge(xk_ready, TASKS - NBLK + p + 1)
                        norm_statistics(n, n % 2, XK[:, p])
                    else:
                        dve.wait_ge(n_out, norm_number(1, p) + 1)
                        dve.wait_ge(x0_in, 16 * (p + 1))
                        nc.vector.tensor_tensor(X1[:, p], X1[:, p], XK[:, p], ALU.add).then_inc(x1_ready, 1)
                        dve.wait_ge(x1_ready, p + 1)
                        norm_statistics(n, n % 2, X1[:, p])

                def dequantise():
                    dve.wait_ge(q_in, 64)
                    nc.vector.tensor_scalar(QW, QI, 1.0 / 7.5, -1.0, ALU.mult, ALU.add).then_inc(dq_step, 1)
                    dve.wait_ge(dq_step, 1)
                    v = QW.rearrange("p w (g c) -> p w g c", c=16)
                    nc.vector.tensor_tensor(v, v, QSC.unsqueeze(3).to_broadcast([128, NW, 8, 16]), ALU.mult) \
                        .then_inc(dq_step, 1)

                def q_step(it):
                    if 0 <= it.base < STEPS_Q:
                        wait(dve, l1_full, it.val(1, 1))
                        if it.base >= 2:
                            wait(dve, n_out, norm_of_step(it, 2) + 1)
                        r = RQ[it.base % 2]
                        nc.vector.tensor_tensor(r[:, :, :], P[:, 2, :].rearrange("p (s e) -> p s e", s=SEQ),
                                                rows(QB, it.val(1, 0) // NBLK * 2), ALU.add).then_inc(l1_added, 1)
                    if it.base + 2 < STEPS_Q:
                        wait(dve, h_ready, it.val(1, 3))
                        wait(dve, ht_full, it.val(1, 2))
                        nc.vector.tensor_copy(HS[:, :, :], XK[:, it.val(1, 2 + NBLK) % NBLK]).then_inc(hs_ready, 1)
                    if 0 <= it.base < STEPS_Q:
                        wait(dve, l1_added, it.val(1, 1))
                        norm_statistics(norm_of_step(it), parity_of_step(it), RQ[it.base % 2])
                    if it.base == 3:
                        dve.wait_ge(n_out, norm_number(2, 7) + 1)
                        dve.memset(CARRY[:, 0:1], 0.0).then_inc(h_ready, 2)
                    if it.base >= 3:
                        wait(dve, l2_full, it.val(1, -2))
                        wait(dve, hb_ready, it.val(1, -2))
                        nc.vector.tensor_tensor(XK[:, it.val(1, NBLK - 3) % NBLK],
                                                P[:, 3, :].rearrange("p (s e) -> p s e", s=SEQ),
                                                HB[:, it.val(1, 1) % 4], ALU.add).then_inc(h_ready, 1)

                def first_h():
                    dve.wait_ge(q_tables_in, 48)
                    dve.wait_ge(av_done, SEQ * TASKS)
                    dve.wait_ge(n_out, norm_number(2, 5) + 1)
                    dve.memset(CARRY[:, 0:1], 0.0).then_inc(h_ready, NBLK - 2)
                    q_step(It(-2))

                def input_lo(blk, n):
                    wait(dve, xh_ready, n)
                    nc.vector.tensor_tensor(XL[:, :], XT[:, blk, :], XH[:, :].bitcast(F32), ALU.subtract) \
                        .then_inc(xl_ready, 1)

                def layers(it):
                    A, B, C, Dd = (it.active(x) for x in "ABCD")
                    if A:
                        emptied(dve, "XD", it.prev())
                        full(dve, "VP", it.prev())
                        dve.memset(CARRY[:, 0:1], 0.0)
                        nc.vector.tensor_copy(XS[:, :], XT[:, it.blk("A"), :]).then_inc(xs_ready, 1)
                    if C:
                        divide(it, 0)
                        divide(it, 1)
                    if it.prev().active("C"):
                        normalise_2(it.prev())
                    if B:
                        mask(it, 0)
                    if it.base < TASKS:
                        for p in FRONT.get(it.base, ()):
                            front(1, p)
                    if C:
                        if it.base == TASKS:
                            dequantise()
                        wait(dve, xk_ready, it.val(1, -1 if it.base <= NBLK else -NBLK))
                        wait(dve, ln_norm, it.val(2, -2))
                        residual(it, "WO", XK[:, it.blk("C")])
                        statistics(it, 1)
                        if it.base == TASKS:
                            first_h()
                            for p in FRONT[TASKS]:
                                front(1, p)
                    if B:
                        mask(it, 1)
                    if C:
                        layer_loaded(dve, it)
                        wait(dve, ln_norm, it.val(2, -1))
                        nc.vector.tensor_tensor(N[:, :, :], N[:, :, :], rows(G1, it.layer("C") % 2), ALU.mult) \
                            .then_inc(ln_gain, 1)
                    if A:
                        if it.base == FIRST:
                            dve.wait_ge(wv_in, 32)
                        values(it)
                    if B:
                        mask(it, 2, (0, 1))
                    if it.base == TASKS:
                        q_step(It(-1))
                    if C:
                        full(dve, "HT", it)
                        wait(dve, hf_hi, it.val(1, 0))
                        nc.vector.tensor_tensor(HFL[:, :], P[:, BANK["HT"], :], HFH[:, :].bitcast(F32),
                                                ALU.subtract).then_inc(drained[BANK["HT"]], 1)
                    if B:
                        mask(it, 2, (2, 3))
                    if B and it.base < TASKS - 1:
                        add_state(it, 0)
                    if A:
                        operands_lo(it, 0)
                        operands_lo(it, 1)
                    for p in FRONT.get(it.base, ())[:1]:
                        front(2, p)
                    if B:
                        mask(it, 3)
                    for p in FRONT.get(it.base, ())[1:]:
                        front(2, p)
                    if A:
                        operands_lo(it, 2)
                        operands_lo(it, 3)
                    if A and it.base + 2 < TASKS:
                        input_lo(it.val(1, 2) % NBLK, it.val(1, 3))
                    if it.base == TASKS:
                        q_step(It(0))
                    if C:
                        wait(dve, h1b_ready, it.val(1, 0))
                        residual(it, "W2", H1B[:, :, :])
                        statistics(it, 2)
                    if B and it.base < TASKS - 1:
                        add_state(it, 1)

                input_lo(0, 1)
                pipeline(dve, layers)

                def add_x1(it):
                    if it.base < NBLK:
                        wait(dve, h_ready, it.val(1, STEPS_Q + 1))
                        norm_statistics(it.val(1, NORM_H), it.base % 2, XK[:, it.val(1, 0)])
                    if it.base >= 2:
                        wait(dve, n_out, it.val(1, NORM_H - 1))
                        nc.vector.tensor_tensor(XK[:, it.val(1, -2)], XK[:, it.val(1, -2)], X1[:, it.val(1, -2)],
                                                ALU.add).then_inc(out_ready, 1)

                normalise_2(It(TASKS))
                q_step(It(1))
                front(1, 7)
                q_step(It(2))
                front(2, 7)
                pairs(dve, 3, *STEADY_Q, STEPS_Q, q_step)
                add_x1(It(0))
                q_step(It(STEPS_Q + 1))
                add_x1(It(1))
                q_step(It(STEPS_Q + 2))
                pairs(dve, 2, 2, NBLK // 2 - 1, NBLK + 1, add_x1)

            @block.gpsimd
            def _(pool):
                def select(t, op, pattern, base, mult, fill, n):
                    pool.wait_ge(consts, n)
                    pool.affine_select(out=t, in_=t, compare_op=op, fill=fill, base=base, pattern=pattern,
                                       channel_multiplier=mult).then_inc(consts, 1)

                def norm_factors(n, par):
                    wait(pool, n_var, 2 * n + 2)
                    wait(pool, n_out, n - 1 if isinstance(n, int) else n + -1)
                    nc.gpsimd.tensor_tensor(NRS[:, par, :], NVE[:, par, :], NHALF[:, :], ALU.pow).then_inc(n_rstd, 1)
                    wait(pool, n_rstd, n + 1)
                    nc.gpsimd.tensor_tensor(NSH[:, par, :], NNM[:, par, :], NRS[:, par, :], ALU.mult) \
                        .then_inc(n_shift, 1)

                pool.memset(IDN[:, :], 0.0).then_inc(consts, 1)
                pool.memset(HM8[:, :], 1.0).then_inc(consts, 1)
                pool.memset(NHALF[:, :], -0.5).then_inc(consts, 1)
                select(IDN[:, :], ALU.not_equal, [[-1, 128]], 0, 1, 1.0, 3)
                for half in range(2):
                    hm = HM8[64 * half:64 * half + 64, :]
                    select(hm, ALU.is_ge, [[-DH, HT_]], 0, 1, 0.0, 4 + 2 * half)
                    select(hm, ALU.is_ge, [[DH, HT_]], DH - 1, -1, 0.0, 5 + 2 * half)

                def input_block(it):
                    if it.base < NBLK:
                        norm_factors(it.val(1, NORM_IN), it.base % 2)
                    if it.base >= 1:
                        wait(pool, n_out, it.val(1, NORM_IN))
                        nc.gpsimd.tensor_tensor(XK[:, it.val(1, -1)], XN[(it.base - 1) % 2][:, :, :], rows(BO, 0),
                                                ALU.add).then_inc(pre_xk, 1)

                pool.wait_ge(consts, 8)
                pool.wait_ge(bo_in, 16)
                pairs(pool, 0, 2, NBLK // 2 - 1, NBLK, input_block)

                pool.memset(TRI[:, :], 1.0).then_inc(consts, 1)
                pool.memset(BDM[:, :], 1.0).then_inc(consts, 1)
                pool.memset(PARM[:, :], 0.0).then_inc(consts, 1)
                pool.memset(KEEP[:, :], 1.0).then_inc(consts, 1)
                bdm = BDM[:, :].rearrange("p (h c) -> p h c", h=HT_)
                select(bdm, ALU.is_ge, [[-SLOT, HT_], [0, SLOT]], 0, 1, 0.0, 12)
                select(bdm, ALU.is_ge, [[SLOT, HT_], [0, SLOT]], SLOT - 1, -1, 0.0, 13)
                for g in range(4):
                    for par in range(2):
                        h = 2 * g + par
                        pool.wait_ge(consts, 14 + 2 * g)
                        pool.tensor_tensor(PARM[:, par:par + 1], PARM[:, par:par + 1],
                                           BDM[:, SLOT * h:SLOT * h + 1], ALU.add).then_inc(consts, 1)
                select(TRI[:, :], ALU.is_ge, [[1, 128]], 0, -1, 0.0, 22)
                pool.memset(KEEP[:, 0:TASKS + 1:NBLK], 0.0).then_inc(consts, 1)
                pool.memset(BO[:, LAYERS, :], 0.0).then_inc(consts, 1)
                pool.wait_ge(zeroed, 3)
                for buf in range(2):
                    for s in range(SEQ):
                        for par in range(2):
                            ones = VP[:, buf, s, par::2, SLOT * par + DEN]
                            pool.memset(ones, 1.0).then_inc(consts, 1)
                pool.wait_ge(consts, ALL_CONSTS)

                def rstd(it, n):
                    wait(pool, ln_var, it.val(2, n - 2))
                    nc.gpsimd.tensor_tensor(RS[:, :], VE[:, :], NHALF[:, :], ALU.pow).then_inc(ln_rstd, 1)
                    if n == 1:
                        wait(pool, ln_nm, it.val(1, 0))
                        wait(pool, ln_rstd, it.val(2, -1))
                        nc.gpsimd.tensor_tensor(SHF[:, :], NM[:, :], RS[:, :], ALU.mult).then_inc(ln_shift, 1)

                def affine(it, n, gain, shift, dst):
                    if n == 2:
                        wait(pool, ln_norm, it.val(2, 0))
                        nc.gpsimd.tensor_tensor(N[:, :, :], N[:, :, :], rows(gain, it.layer("C") % 2), ALU.mult) \
                            .then_inc(ln_gain, 1)
                    wait(pool, ln_gain, it.val(2, n - 2))
                    nc.gpsimd.tensor_tensor(dst, N[:, :, :], rows(shift, it.layer("C") % 2), ALU.add) \
                        .then_inc(ln_out, 1)
                    wait(pool, ln_out, it.val(2, n - 2))

                def mask_state(it, j):
                    wait(pool, state_added, it.val(2, 1 + j))
                    wait(pool, keep_ready, it.val(1, 1))
                    nc.gpsimd.tensor_tensor(SK[:, 2 * j:2 * j + 2].rearrange("p a b c -> p (a b) c"),
                                            SF[:, 2 * j:2 * j + 2].rearrange("p a b c -> p (a b) c"),
                                            MK[:, :].unsqueeze(1).to_broadcast([128, 4, 128]),
                                            ALU.mult).then_inc(state_ready, 1)

                def q_step(it):
                    wait(pool, h_ready, it.val(1, 5 if it.base >= 4 else 1))
                    nc.gpsimd.tensor_tensor(HB[:, it.val(1, 0) % 4], XK[:, it.val(1, 0) % NBLK],
                                            rows(QB, it.val(1, 0) // NBLK * 2 + 1), ALU.add).then_inc(hb_ready, 1)
                    norm_factors(norm_of_step(it), parity_of_step(it))

                def weights_lo(l, n):
                    wait(pool, wa_ready, 2 * n)
                    nc.gpsimd.tensor_tensor(CAL[:, :], WA[:, l, 0:256], CAH[:, :].bitcast(F32), ALU.subtract) \
                        .then_inc(wal_ready, 1)

                def layers(it):
                    A, B, C, Dd = (it.active(x) for x in "ABCD")
                    if it.base == 1:
                        pool.wait_ge(w_in, W_DMAS)
                    if it.base < TASKS:
                        for p in FRONT.get(it.base, ()):
                            norm_factors(norm_number(1, p), norm_number(1, p) % 2)
                    if C:
                        layer_loaded(pool, it)
                        rstd(it, 1)
                    if it.base == TASKS:
                        for p in FRONT[TASKS]:
                            norm_factors(norm_number(1, p), norm_number(1, p) % 2)
                    if C:
                        affine(it, 1, G1, BE1, H1[:, :, :])
                        nc.gpsimd.tensor_tensor(H1B[:, :, :], H1[:, :, :], rows(BF2, it.layer("C") % 2), ALU.add) \
                            .then_inc(h1b_ready, 1)
                    if B and it.base < TASKS - 1:
                        nc.gpsimd.tensor_tensor(MK[:, :], BDM[:, :],
                                                KEEP[:, bass.ds(it.val(1, 1), 1)].to_broadcast([128, 128]),
                                                ALU.mult).then_inc(keep_ready, 1)
                    if A and it.base + 2 < TASKS:
                        weights_lo(it.val(1, 2) // NBLK, it.val(1, 3))
                    if B and it.base < TASKS - 1:
                        mask_state(it, 0)
                    for p in FRONT.get(it.base, ()):
                        norm_factors(norm_number(2, p), norm_number(2, p) % 2)
                    if it.base == TASKS:
                        pool.wait_ge(q_tables_in, 48)
                        pool.wait_ge(av_done, SEQ * TASKS)
                        q_step(It(0))
                    if C:
                        rstd(it, 2)
                    if B and it.base < TASKS - 1:
                        mask_state(it, 1)
                    if C:
                        affine(it, 2, G2, BE2, X2[:, :, :])
                        nc.gpsimd.tensor_tensor(XK[:, it.blk("C")], X2[:, :, :],
                                                rows(BO, it.val(1, -1) // NBLK + 1), ALU.add).then_inc(xk_ready, 1)
                    if B:
                        wait(pool, wc_ready, it.val(2, 2))
                        nc.gpsimd.tensor_tensor(CCL[:, :], WC[:, it.val(1, 0) // NBLK, 0:FF], CCH[:, :].bitcast(F32),
                                                ALU.subtract).then_inc(wcl_ready, 1)

                weights_lo(0, 1)
                pipeline(pool, layers)

                def factors_h(it):
                    norm_factors(it.val(1, NORM_H), it.base % 2)

                q_step(It(1))
                norm_factors(norm_number(1, 7), norm_number(1, 7) % 2)
                q_step(It(2))
                norm_factors(norm_number(2, 7), norm_number(2, 7) % 2)
                pairs(pool, 3, 4, (STEPS_Q - 4) // 2, STEPS_Q - 1, q_step)
                pairs(pool, 0, 2, NBLK // 2 - 1, NBLK - 1, factors_h)


_INS = ["L0_attn_x", "L0_attn_Wq", "L0_attn_bq", "L0_attn_Wk", "L0_attn_bk", "L0_attn_Wv", "L0_attn_bv",
        "L0_attn_Wo", "L0_attn_bo", "L0_attn_omega", "L0_attn_g1", "L0_attn_be1", "L0_attn_W1", "L0_attn_bf1",
        "L0_attn_W2", "L0_attn_bf2", "L0_attn_g2", "L0_attn_be2", "L0_ffn_qweights", "L0_ffn_scales",
        "L0_ffn_biases", "L0_ffn_lora_a", "L0_ffn_lora_b", "L0_ffn_ln_gamma", "L0_ffn_ln_beta"]
_OUTS = [((4, 1024, 128), "float32")]


def kernel(**inputs):
    import numpy as _np
    import concourse.bacc as _bacc
    from concourse import mybir as _mybir
    from concourse.bass_utils import run_bass_kernel_spmd as _run

    nc = _bacc.Bacc("TRN2", target_bir_lowering=False, num_devices=1)
    arrays, args = {}, []
    for name in _INS:
        a = _np.ascontiguousarray(inputs[name])
        arrays[f"in_{name}_dram"] = a
        args.append(nc.dram_tensor(f"in_{name}_dram", a.shape, _mybir.dt.from_np(a.dtype), kind="ExternalInput").ap())
    for i, (shape, dtype) in enumerate(_OUTS):
        dt = _mybir.dt.from_np(_np.dtype(dtype))
        args.append(nc.dram_tensor(f"out_{i}_dram", shape, dt, kind="ExternalOutput").ap())
    sandwich(nc, *args)
    r = _run(nc, [arrays], core_ids=[0])
    got = tuple(r.results[0][f"out_{i}_dram"] for i in range(len(_OUTS)))
    return got[0]
```
